# Optimizing a Trainium2 kernel written in Bass

```python
import numpy as np
import jax
import jax.numpy as jnp

def _softmax(x, axis=-1):
    return jax.nn.softmax(x, axis=axis)
def _gelu(x):
    return jax.nn.gelu(x, approximate=True)
def _silu(x):
    return jax.nn.silu(x)
def _sigmoid(x):
    return jax.nn.sigmoid(x)
def _layernorm(x, axis=-1, eps=1e-5):
    m = jnp.mean(x, axis=axis, keepdims=True)
    v = jnp.var(x, axis=axis, keepdims=True)
    return (x - m) / jnp.sqrt(v + eps)
def _scatter_add(tgt, idx, src, axis=0):
    return tgt.at[idx].add(src)
def _segment_sum(src, seg, n):
    return jax.ops.segment_sum(src, seg, n)

kernel_name = 'mk_conv_preact_d4_conv_nchw128_eadcc3'

def setup_inputs(seed: int = 0):
    np.random.seed(seed)
    _w = jnp.asarray
    def _rec_inputs():
        import jax
        import jax.numpy as jnp
        _gk = jax.random.key(seed)
        x = -0.0002928 + 1 * jax.random.normal(jax.random.fold_in(_gk, 1), (32, 128, 32, 32), jnp.float32)
        return x
    x = _rec_inputs()
    def _L0_conv_setup():
        import jax, jax.numpy as jnp
        import numpy as np
        PAD = 1
        key = jax.random.key(seed)
        k1, k2, k3 = jax.random.split(key, 3)
        N, C, F, H, W, HH, WW = (32, 128, 128, 32, 32, 3, 3)
        x = jax.random.normal(k1, (N, C, H, W), dtype=jnp.float32)
        weight = jax.random.normal(k2, (F, C, HH, WW), dtype=jnp.float32) * 0.05
        bias = jax.random.normal(k3, (F,), dtype=jnp.float32) * 0.05
        return {'x': x, 'weight': weight, 'bias': bias}
    _L0_conv_all = _L0_conv_setup()
    _L0_conv_in = {k: v for k, v in _L0_conv_all.items() if k in ('weight', 'bias', )}
    del _L0_conv_all

    def _L1_conv_setup():
        import jax, jax.numpy as jnp
        import numpy as np
        DIM = 128
        D_STATE = 16
        D_CONV = 4
        EXPAND = 2
        D_INNER = DIM * EXPAND
        DT_RANK = (DIM + 15) // 16
        B = 4
        H = 64
        W = 64
        EPS = 1e-05

        def _bn(x, g, b, m, v):
            scale = g / jnp.sqrt(v + EPS)
            return x * scale[None, :, None, None] + (b - m * scale)[None, :, None, None]

        def _mamba(x, in_proj_w, conv_w, conv_b, x_proj_w, dt_proj_w, dt_proj_b, A_log, Dp, out_proj_w):
            Bm, L, C = x.shape
            xz = jnp.einsum('blc,ic->bli', x, in_proj_w)
            u, z = jnp.split(xz, 2, axis=-1)
            xp = jnp.pad(u, ((0, 0), (D_CONV - 1, 0), (0, 0)))
            uc = sum((xp[:, k:k + L, :] * conv_w[:, k] for k in range(D_CONV))) + conv_b
            uc = jax.nn.silu(uc)
            dbl = jnp.einsum('bld,id->bli', uc, x_proj_w)
            dtr = dbl[..., :DT_RANK]
            Bt = dbl[..., DT_RANK:DT_RANK + D_STATE]
            Ct = dbl[..., DT_RANK + D_STATE:]
            dt = jax.nn.softplus(jnp.einsum('blr,dr->bld', dtr, dt_proj_w) + dt_proj_b)
            A = -jnp.exp(A_log)

            def step(h, inp):
                dt_t, B_t, C_t, u_t = inp
                dA = jnp.exp(dt_t[..., None] * A)
                h = dA * h + (dt_t * u_t)[..., None] * B_t[:, None, :]
                y = jnp.einsum('bdn,bn->bd', h, C_t)
                return (h, y)
            h0 = jnp.zeros((Bm, D_INNER, D_STATE), x.dtype)
            xs = (dt.transpose(1, 0, 2), Bt.transpose(1, 0, 2), Ct.transpose(1, 0, 2), uc.transpose(1, 0, 2))
            _, ys = jax.lax.scan(step, h0, xs)
            y = ys.transpose(1, 0, 2) + uc * Dp
            y = y * jax.nn.silu(z)
            return jnp.einsum('bld,od->blo', y, out_proj_w)
        key = jax.random.key(seed)
        ks = jax.random.split(key, 12)

        def n(k, shape, s=0.02):
            return jax.random.normal(k, shape, jnp.float32) * s
        return {'x': jax.random.normal(ks[0], (B, DIM, H, W), jnp.float32), 'nin_w': n(ks[1], (DIM, DIM)), 'bn1_g': jnp.ones((DIM,), jnp.float32), 'bn1_b': jnp.zeros((DIM,), jnp.float32), 'bn1_m': jnp.zeros((DIM,), jnp.float32), 'bn1_v': jnp.ones((DIM,), jnp.float32), 'in_proj_w': n(ks[2], (2 * D_INNER, DIM)), 'conv_w': n(ks[3], (D_INNER, D_CONV), 0.2), 'conv_b': jnp.zeros((D_INNER,), jnp.float32), 'x_proj_w': n(ks[4], (DT_RANK + 2 * D_STATE, D_INNER)), 'dt_proj_w': n(ks[5], (D_INNER, DT_RANK), 0.1), 'dt_proj_b': jnp.full((D_INNER,), -4.6, jnp.float32) + n(ks[6], (D_INNER,), 0.1), 'A_log': jnp.log(jnp.broadcast_to(jnp.arange(1, D_STATE + 1, dtype=jnp.float32), (D_INNER, D_STATE))), 'D': jnp.ones((D_INNER,), jnp.float32), 'out_proj_w': n(ks[7], (DIM, D_INNER)), 'nin2_w': n(ks[8], (DIM, DIM)), 'bn2_g': jnp.ones((DIM,), jnp.float32), 'bn2_b': jnp.zeros((DIM,), jnp.float32), 'bn2_m': jnp.zeros((DIM,), jnp.float32), 'bn2_v': jnp.ones((DIM,), jnp.float32)}
    _L1_conv_all = _L1_conv_setup()
    _L1_conv_in = {k: v for k, v in _L1_conv_all.items() if k in ('nin_w', 'bn1_g', 'bn1_b', 'bn1_m', 'bn1_v', 'in_proj_w', 'conv_w', 'conv_b', 'x_proj_w', 'dt_proj_w', 'dt_proj_b', 'A_log', 'D', 'out_proj_w', 'nin2_w', 'bn2_g', 'bn2_b', 'bn2_m', 'bn2_v', )}
    del _L1_conv_all

    def _L2_conv_setup():
        import jax, jax.numpy as jnp
        import numpy as np
        from jax import lax

        def _c1x1(t, w, b=None):
            y = jnp.einsum('bchw,oc->bohw', t, w)
            if b is not None:
                y = y + b[None, :, None, None]
            return y

        def _mamba(u, in_w, conv_w, conv_b, xproj_w, dt_w, dt_b, A_log, Dp, out_w):
            B, L, _ = u.shape
            d_inner = conv_w.shape[0]
            d_state = A_log.shape[1]
            dt_rank = dt_w.shape[1]
            d_conv = conv_w.shape[2]
            xz = jnp.einsum('bld,ed->ble', u, in_w)
            xc, z = (xz[..., :d_inner], xz[..., d_inner:])
            xt = jnp.pad(xc.transpose(0, 2, 1), ((0, 0), (0, 0), (d_conv - 1, 0)))
            xt = lax.conv_general_dilated(xt, conv_w, (1,), 'VALID', feature_group_count=d_inner, dimension_numbers=('NCH', 'OIH', 'NCH'))
            xc = jax.nn.silu(xt + conv_b[None, :, None]).transpose(0, 2, 1)
            dbc = jnp.einsum('bld,ed->ble', xc, xproj_w)
            dt = dbc[..., :dt_rank]
            B_ = dbc[..., dt_rank:dt_rank + d_state]
            C_ = dbc[..., dt_rank + d_state:]
            delta = jax.nn.softplus(jnp.einsum('blr,dr->bld', dt, dt_w) + dt_b)
            A = -jnp.exp(A_log)
            dA = jnp.exp(delta[..., None] * A)
            dBu = delta[..., None] * B_[:, :, None, :] * xc[..., None]

            def step(h, inp):
                dA_t, dBu_t, c_t = inp
                h = dA_t * h + dBu_t
                y = jnp.einsum('bdn,bn->bd', h, c_t)
                return (h, y)
            h0 = jnp.zeros((B, d_inner, d_state), dtype=u.dtype)
            _, ys = lax.scan(step, h0, (dA.transpose(1, 0, 2, 3), dBu.transpose(1, 0, 2, 3), C_.transpose(1, 0, 2)))
            y = ys.transpose(1, 0, 2) + xc * Dp
            y = y * jax.nn.silu(z)
            return jnp.einsum('bld,od->blo', y, out_w)
        key = jax.random.key(seed)
        B, C, H, W = (8, 128, 160, 160)
        mip, d_in, d_st, d_r, d_cv = (8, 256, 16, 8, 4)
        ks = iter(jax.random.split(key, 64))

        def rn(shape, s=0.05):
            return jax.random.normal(next(ks), shape, dtype=jnp.float32) * s
        inp = {'x': jax.random.normal(next(ks), (B, C, H, W), dtype=jnp.float32)}
        inp.update(conv1_w=rn((mip, C)), conv1_b=rn((mip,)), bn_g=jnp.ones((mip,)), bn_b=jnp.zeros((mip,)), bn_m=jnp.zeros((mip,)), bn_v=jnp.ones((mip,)), convh_w=rn((C, mip)), convh_b=rn((C,)), convw_w=rn((C, mip)), convw_b=rn((C,)), mlpx_w1=rn((C, C)), mlpx_b1=rn((C,)), mlpx_w2=rn((C, C)), mlpx_b2=rn((C,)), mlpy_w1=rn((C, C)), mlpy_b1=rn((C,)), mlpy_w2=rn((C, C)), mlpy_b2=rn((C,)), adjust_w=rn((C, 2 * C)))
        for p in ('mx', 'my'):
            inp[p + '_in_w'] = rn((2 * d_in, C))
            inp[p + '_conv_w'] = rn((d_in, 1, d_cv), 0.3)
            inp[p + '_conv_b'] = rn((d_in,))
            inp[p + '_xproj_w'] = rn((d_r + 2 * d_st, d_in))
            inp[p + '_dt_w'] = rn((d_in, d_r))
            inp[p + '_dt_b'] = rn((d_in,))
            inp[p + '_Alog'] = jnp.log(jnp.broadcast_to(jnp.arange(1, d_st + 1, dtype=jnp.float32), (d_in, d_st)))
            inp[p + '_D'] = jnp.ones((d_in,))
            inp[p + '_out_w'] = rn((C, d_in))
        return inp
    _L2_conv_all = _L2_conv_setup()
    _L2_conv_in = {k: v for k, v in _L2_conv_all.items() if k in ('conv1_w', 'conv1_b', 'bn_g', 'bn_b', 'bn_m', 'bn_v', 'convh_w', 'convh_b', 'convw_w', 'convw_b', 'mlpx_w1', 'mlpx_b1', 'mlpx_w2', 'mlpx_b2', 'mlpy_w1', 'mlpy_b1', 'mlpy_w2', 'mlpy_b2', 'adjust_w', 'mx_in_w', 'mx_conv_w', 'mx_conv_b', 'mx_xproj_w', 'mx_dt_w', 'mx_dt_b', 'mx_Alog', 'mx_D', 'mx_out_w', 'my_in_w', 'my_conv_w', 'my_conv_b', 'my_xproj_w', 'my_dt_w', 'my_dt_b', 'my_Alog', 'my_D', 'my_out_w', )}
    del _L2_conv_all

    def _L3_conv_setup():
        import jax, jax.numpy as jnp
        import numpy as np
        NQ = 4
        NL = 2

        def _apply_1q(state, U, w):
            state = jnp.moveaxis(state, w + 1, -1)
            state = jnp.einsum('ij,...j->...i', U, state)
            return jnp.moveaxis(state, -1, w + 1)

        def _apply_cnot(state, cw, tw):
            s0 = jnp.take(state, jnp.array([0]), axis=cw + 1)
            s1 = jnp.take(state, jnp.array([1]), axis=cw + 1)
            s1 = jnp.flip(s1, axis=tw + 1)
            return jnp.concatenate([s0, s1], axis=cw + 1)

        def _simulate(xq, qw):
            half = 0.5 * jnp.pi * xq
            c, s = (jnp.cos(half), jnp.sin(half))
            state = jnp.stack([c[:, 0], s[:, 0]], axis=-1).astype(jnp.complex64)
            for w in range(1, NQ):
                q = jnp.stack([c[:, w], s[:, w]], axis=-1).astype(jnp.complex64)
                state = jnp.einsum('b...,bj->b...j', state, q)
            for l in range(NL):
                for w in range(NQ):
                    phi, theta, omega = (qw[l, w, 0], qw[l, w, 1], qw[l, w, 2])
                    ct = jnp.cos(0.5 * theta)
                    st = jnp.sin(0.5 * theta)
                    a = 0.5 * (phi + omega)
                    b = 0.5 * (phi - omega)
                    row0 = jnp.stack([jnp.exp(-1j * a) * ct, -jnp.exp(1j * b) * st])
                    row1 = jnp.stack([jnp.exp(-1j * b) * st, jnp.exp(1j * a) * ct])
                    U = jnp.stack([row0, row1]).astype(jnp.complex64)
                    state = _apply_1q(state, U, w)
                r = l % (NQ - 1) + 1
                for w in range(NQ):
                    state = _apply_cnot(state, w, (w + r) % NQ)
            p = state.real ** 2 + state.imag ** 2
            ez = []
            for w in range(NQ):
                axes = tuple((a for a in range(1, NQ + 1) if a != w + 1))
                m = p.sum(axis=axes)
                ez.append(m[:, 0] - m[:, 1])
            return jnp.stack(ez, axis=1)
        key = jax.random.key(seed)
        ks = jax.random.split(key, 6)
        N, C, H, W, OUT = (8, 128, 128, 128, 128)
        x = jax.random.normal(ks[0], (N, C, H, W), dtype=jnp.float32)
        pre_w = jax.random.normal(ks[1], (NQ, C), dtype=jnp.float32) * (1.0 / np.sqrt(C))
        pre_b = jax.random.normal(ks[2], (NQ,), dtype=jnp.float32) * 0.01
        q_weights = jax.random.normal(ks[3], (NL, NQ, 3), dtype=jnp.float32)
        post_w = jax.random.normal(ks[4], (OUT, NQ), dtype=jnp.float32) * 0.5
        post_b = jax.random.normal(ks[5], (OUT,), dtype=jnp.float32) * 0.01
        return {'x': x, 'pre_w': pre_w, 'pre_b': pre_b, 'q_weights': q_weights, 'post_w': post_w, 'post_b': post_b}
    _L3_conv_all = _L3_conv_setup()
    _L3_conv_in = {k: v for k, v in _L3_conv_all.items() if k in ('pre_w', 'pre_b', 'q_weights', 'post_w', 'post_b', )}
    del _L3_conv_all

    return {
        "x": x,
        "L0_conv_weight": _L0_conv_in["weight"],
        "L0_conv_bias": _L0_conv_in["bias"],
        "L1_conv_nin_w": _L1_conv_in["nin_w"],
        "L1_conv_bn1_g": _L1_conv_in["bn1_g"],
        "L1_conv_bn1_b": _L1_conv_in["bn1_b"],
        "L1_conv_bn1_m": _L1_conv_in["bn1_m"],
        "L1_conv_bn1_v": _L1_conv_in["bn1_v"],
        "L1_conv_in_proj_w": _L1_conv_in["in_proj_w"],
        "L1_conv_conv_w": _L1_conv_in["conv_w"],
        "L1_conv_conv_b": _L1_conv_in["conv_b"],
        "L1_conv_x_proj_w": _L1_conv_in["x_proj_w"],
        "L1_conv_dt_proj_w": _L1_conv_in["dt_proj_w"],
        "L1_conv_dt_proj_b": _L1_conv_in["dt_proj_b"],
        "L1_conv_A_log": _L1_conv_in["A_log"],
        "L1_conv_D": _L1_conv_in["D"],
        "L1_conv_out_proj_w": _L1_conv_in["out_proj_w"],
        "L1_conv_nin2_w": _L1_conv_in["nin2_w"],
        "L1_conv_bn2_g": _L1_conv_in["bn2_g"],
        "L1_conv_bn2_b": _L1_conv_in["bn2_b"],
        "L1_conv_bn2_m": _L1_conv_in["bn2_m"],
        "L1_conv_bn2_v": _L1_conv_in["bn2_v"],
        "L2_conv_conv1_w": _L2_conv_in["conv1_w"],
        "L2_conv_conv1_b": _L2_conv_in["conv1_b"],
        "L2_conv_bn_g": _L2_conv_in["bn_g"],
        "L2_conv_bn_b": _L2_conv_in["bn_b"],
        "L2_conv_bn_m": _L2_conv_in["bn_m"],
        "L2_conv_bn_v": _L2_conv_in["bn_v"],
        "L2_conv_convh_w": _L2_conv_in["convh_w"],
        "L2_conv_convh_b": _L2_conv_in["convh_b"],
        "L2_conv_convw_w": _L2_conv_in["convw_w"],
        "L2_conv_convw_b": _L2_conv_in["convw_b"],
        "L2_conv_mlpx_w1": _L2_conv_in["mlpx_w1"],
        "L2_conv_mlpx_b1": _L2_conv_in["mlpx_b1"],
        "L2_conv_mlpx_w2": _L2_conv_in["mlpx_w2"],
        "L2_conv_mlpx_b2": _L2_conv_in["mlpx_b2"],
        "L2_conv_mlpy_w1": _L2_conv_in["mlpy_w1"],
        "L2_conv_mlpy_b1": _L2_conv_in["mlpy_b1"],
        "L2_conv_mlpy_w2": _L2_conv_in["mlpy_w2"],
        "L2_conv_mlpy_b2": _L2_conv_in["mlpy_b2"],
        "L2_conv_adjust_w": _L2_conv_in["adjust_w"],
        "L2_conv_mx_in_w": _L2_conv_in["mx_in_w"],
        "L2_conv_mx_conv_w": _L2_conv_in["mx_conv_w"],
        "L2_conv_mx_conv_b": _L2_conv_in["mx_conv_b"],
        "L2_conv_mx_xproj_w": _L2_conv_in["mx_xproj_w"],
        "L2_conv_mx_dt_w": _L2_conv_in["mx_dt_w"],
        "L2_conv_mx_dt_b": _L2_conv_in["mx_dt_b"],
        "L2_conv_mx_Alog": _L2_conv_in["mx_Alog"],
        "L2_conv_mx_D": _L2_conv_in["mx_D"],
        "L2_conv_mx_out_w": _L2_conv_in["mx_out_w"],
        "L2_conv_my_in_w": _L2_conv_in["my_in_w"],
        "L2_conv_my_conv_w": _L2_conv_in["my_conv_w"],
        "L2_conv_my_conv_b": _L2_conv_in["my_conv_b"],
        "L2_conv_my_xproj_w": _L2_conv_in["my_xproj_w"],
        "L2_conv_my_dt_w": _L2_conv_in["my_dt_w"],
        "L2_conv_my_dt_b": _L2_conv_in["my_dt_b"],
        "L2_conv_my_Alog": _L2_conv_in["my_Alog"],
        "L2_conv_my_D": _L2_conv_in["my_D"],
        "L2_conv_my_out_w": _L2_conv_in["my_out_w"],
        "L3_conv_pre_w": _L3_conv_in["pre_w"],
        "L3_conv_pre_b": _L3_conv_in["pre_b"],
        "L3_conv_q_weights": _L3_conv_in["q_weights"],
        "L3_conv_post_w": _L3_conv_in["post_w"],
        "L3_conv_post_b": _L3_conv_in["post_b"],
    }

def reference(x, L0_conv_weight, L0_conv_bias, L1_conv_nin_w, L1_conv_bn1_g, L1_conv_bn1_b, L1_conv_bn1_m, L1_conv_bn1_v, L1_conv_in_proj_w, L1_conv_conv_w, L1_conv_conv_b, L1_conv_x_proj_w, L1_conv_dt_proj_w, L1_conv_dt_proj_b, L1_conv_A_log, L1_conv_D, L1_conv_out_proj_w, L1_conv_nin2_w, L1_conv_bn2_g, L1_conv_bn2_b, L1_conv_bn2_m, L1_conv_bn2_v, L2_conv_conv1_w, L2_conv_conv1_b, L2_conv_bn_g, L2_conv_bn_b, L2_conv_bn_m, L2_conv_bn_v, L2_conv_convh_w, L2_conv_convh_b, L2_conv_convw_w, L2_conv_convw_b, L2_conv_mlpx_w1, L2_conv_mlpx_b1, L2_conv_mlpx_w2, L2_conv_mlpx_b2, L2_conv_mlpy_w1, L2_conv_mlpy_b1, L2_conv_mlpy_w2, L2_conv_mlpy_b2, L2_conv_adjust_w, L2_conv_mx_in_w, L2_conv_mx_conv_w, L2_conv_mx_conv_b, L2_conv_mx_xproj_w, L2_conv_mx_dt_w, L2_conv_mx_dt_b, L2_conv_mx_Alog, L2_conv_mx_D, L2_conv_mx_out_w, L2_conv_my_in_w, L2_conv_my_conv_w, L2_conv_my_conv_b, L2_conv_my_xproj_w, L2_conv_my_dt_w, L2_conv_my_dt_b, L2_conv_my_Alog, L2_conv_my_D, L2_conv_my_out_w, L3_conv_pre_w, L3_conv_pre_b, L3_conv_q_weights, L3_conv_post_w, L3_conv_post_b):
    import jax
    import jax.numpy as jnp
    def _L0_conv_ref(x, weight, bias):
        import jax, jax.numpy as jnp
        import numpy as np
        PAD = 1
        N, C, H, W = x.shape
        F, _, HH, WW = weight.shape
        pad = PAD
        out_H = H - HH + 1 + 2 * pad
        out_W = W - WW + 1 + 2 * pad
        HHH = max(out_H, HH)
        WWW = max(out_W, WW)
        init_H = H + 2 * pad + HHH - 1
        init_W = W + 2 * pad + WWW - 1
        xp = jnp.pad(x, ((0, 0), (0, 0), (pad, init_H - pad - H), (pad, init_W - pad - W)))
        wp = jnp.pad(weight, ((0, 0), (0, 0), (0, init_H - HH), (0, init_W - WW)))
        xf = jnp.fft.rfft2(xp)
        wf = jnp.fft.rfft2(wp)
        of = jnp.einsum('nchw,fchw->nfhw', xf, jnp.conj(wf))
        out = jnp.fft.irfft2(of, s=(init_H, init_W))[..., :out_H, :out_W]
        return out + bias[None, :, None, None]

    def _L1_conv_ref(x, nin_w, bn1_g, bn1_b, bn1_m, bn1_v, in_proj_w, conv_w, conv_b, x_proj_w, dt_proj_w, dt_proj_b, A_log, D, out_proj_w, nin2_w, bn2_g, bn2_b, bn2_m, bn2_v):
        import jax, jax.numpy as jnp
        import numpy as np
        DIM = 128
        D_STATE = 16
        D_CONV = 4
        EXPAND = 2
        D_INNER = DIM * EXPAND
        DT_RANK = (DIM + 15) // 16
        B = 4
        H = 64
        W = 64
        EPS = 1e-05

        def _bn(x, g, b, m, v):
            scale = g / jnp.sqrt(v + EPS)
            return x * scale[None, :, None, None] + (b - m * scale)[None, :, None, None]

        def _mamba(x, in_proj_w, conv_w, conv_b, x_proj_w, dt_proj_w, dt_proj_b, A_log, Dp, out_proj_w):
            Bm, L, C = x.shape
            xz = jnp.einsum('blc,ic->bli', x, in_proj_w)
            u, z = jnp.split(xz, 2, axis=-1)
            xp = jnp.pad(u, ((0, 0), (D_CONV - 1, 0), (0, 0)))
            uc = sum((xp[:, k:k + L, :] * conv_w[:, k] for k in range(D_CONV))) + conv_b
            uc = jax.nn.silu(uc)
            dbl = jnp.einsum('bld,id->bli', uc, x_proj_w)
            dtr = dbl[..., :DT_RANK]
            Bt = dbl[..., DT_RANK:DT_RANK + D_STATE]
            Ct = dbl[..., DT_RANK + D_STATE:]
            dt = jax.nn.softplus(jnp.einsum('blr,dr->bld', dtr, dt_proj_w) + dt_proj_b)
            A = -jnp.exp(A_log)

            def step(h, inp):
                dt_t, B_t, C_t, u_t = inp
                dA = jnp.exp(dt_t[..., None] * A)
                h = dA * h + (dt_t * u_t)[..., None] * B_t[:, None, :]
                y = jnp.einsum('bdn,bn->bd', h, C_t)
                return (h, y)
            h0 = jnp.zeros((Bm, D_INNER, D_STATE), x.dtype)
            xs = (dt.transpose(1, 0, 2), Bt.transpose(1, 0, 2), Ct.transpose(1, 0, 2), uc.transpose(1, 0, 2))
            _, ys = jax.lax.scan(step, h0, xs)
            y = ys.transpose(1, 0, 2) + uc * Dp
            y = y * jax.nn.silu(z)
            return jnp.einsum('bld,od->blo', y, out_proj_w)
        Bb, C, Hh, Ww = x.shape
        h1 = jax.nn.relu(_bn(jnp.einsum('bchw,oc->bohw', x, nin_w), bn1_g, bn1_b, bn1_m, bn1_v))
        L = Hh * Ww
        xf = h1.reshape(Bb, C, L).transpose(0, 2, 1)
        v0 = xf
        v1 = jnp.flip(xf, axis=2)
        v2 = jnp.flip(xf, axis=1)
        v3 = jnp.flip(xf, axis=(1, 2))
        xs = jnp.concatenate([v0, v1, v2, v3], axis=0)
        ym = _mamba(xs, in_proj_w, conv_w, conv_b, x_proj_w, dt_proj_w, dt_proj_b, A_log, D, out_proj_w)
        y0, y1, y2, y3 = jnp.split(ym, 4, axis=0)
        y = (y0 + jnp.flip(y1, axis=2) + jnp.flip(y2, axis=1) + jnp.flip(y3, axis=(1, 2))) / 4
        out = y.transpose(0, 2, 1).reshape(Bb, C, Hh, Ww) + h1
        out = jax.nn.relu(_bn(jnp.einsum('bchw,oc->bohw', out, nin2_w), bn2_g, bn2_b, bn2_m, bn2_v))
        return out

    def _L2_conv_ref(x, conv1_w, conv1_b, bn_g, bn_b, bn_m, bn_v, convh_w, convh_b, convw_w, convw_b, mlpx_w1, mlpx_b1, mlpx_w2, mlpx_b2, mlpy_w1, mlpy_b1, mlpy_w2, mlpy_b2, adjust_w, mx_in_w, mx_conv_w, mx_conv_b, mx_xproj_w, mx_dt_w, mx_dt_b, mx_Alog, mx_D, mx_out_w, my_in_w, my_conv_w, my_conv_b, my_xproj_w, my_dt_w, my_dt_b, my_Alog, my_D, my_out_w):
        import jax, jax.numpy as jnp
        import numpy as np
        from jax import lax

        def _c1x1(t, w, b=None):
            y = jnp.einsum('bchw,oc->bohw', t, w)
            if b is not None:
                y = y + b[None, :, None, None]
            return y

        def _mamba(u, in_w, conv_w, conv_b, xproj_w, dt_w, dt_b, A_log, Dp, out_w):
            B, L, _ = u.shape
            d_inner = conv_w.shape[0]
            d_state = A_log.shape[1]
            dt_rank = dt_w.shape[1]
            d_conv = conv_w.shape[2]
            xz = jnp.einsum('bld,ed->ble', u, in_w)
            xc, z = (xz[..., :d_inner], xz[..., d_inner:])
            xt = jnp.pad(xc.transpose(0, 2, 1), ((0, 0), (0, 0), (d_conv - 1, 0)))
            xt = lax.conv_general_dilated(xt, conv_w, (1,), 'VALID', feature_group_count=d_inner, dimension_numbers=('NCH', 'OIH', 'NCH'))
            xc = jax.nn.silu(xt + conv_b[None, :, None]).transpose(0, 2, 1)
            dbc = jnp.einsum('bld,ed->ble', xc, xproj_w)
            dt = dbc[..., :dt_rank]
            B_ = dbc[..., dt_rank:dt_rank + d_state]
            C_ = dbc[..., dt_rank + d_state:]
            delta = jax.nn.softplus(jnp.einsum('blr,dr->bld', dt, dt_w) + dt_b)
            A = -jnp.exp(A_log)
            dA = jnp.exp(delta[..., None] * A)
            dBu = delta[..., None] * B_[:, :, None, :] * xc[..., None]

            def step(h, inp):
                dA_t, dBu_t, c_t = inp
                h = dA_t * h + dBu_t
                y = jnp.einsum('bdn,bn->bd', h, c_t)
                return (h, y)
            h0 = jnp.zeros((B, d_inner, d_state), dtype=u.dtype)
            _, ys = lax.scan(step, h0, (dA.transpose(1, 0, 2, 3), dBu.transpose(1, 0, 2, 3), C_.transpose(1, 0, 2)))
            y = ys.transpose(1, 0, 2) + xc * Dp
            y = y * jax.nn.silu(z)
            return jnp.einsum('bld,od->blo', y, out_w)
        B, C, H, W = x.shape
        gelu = lambda t: jax.nn.gelu(t, approximate=False)
        x_h = x.mean(3, keepdims=True)
        x_w = x.mean(2, keepdims=True).transpose(0, 1, 3, 2)
        y = jnp.concatenate([x_h, x_w], axis=2)
        y = _c1x1(y, conv1_w, conv1_b)
        y = (y - bn_m[None, :, None, None]) * jax.lax.rsqrt(bn_v + 1e-05)[None, :, None, None]
        y = y * bn_g[None, :, None, None] + bn_b[None, :, None, None]
        y = gelu(y)
        a_h = _c1x1(y[:, :, :H], convh_w, convh_b)
        a_w = _c1x1(y[:, :, H:].transpose(0, 1, 3, 2), convw_w, convw_b)
        ux = x.mean(3).transpose(0, 2, 1)
        x_x = _mamba(ux, mx_in_w, mx_conv_w, mx_conv_b, mx_xproj_w, mx_dt_w, mx_dt_b, mx_Alog, mx_D, mx_out_w)
        x_x = x_x.transpose(0, 2, 1)[..., None]
        x_x = jax.nn.sigmoid(x_x + a_h)
        x_x = _c1x1(gelu(_c1x1(x_x, mlpx_w1, mlpx_b1)), mlpx_w2, mlpx_b2)
        uy = x.mean(2).transpose(0, 2, 1)
        x_y = _mamba(uy, my_in_w, my_conv_w, my_conv_b, my_xproj_w, my_dt_w, my_dt_b, my_Alog, my_D, my_out_w)
        x_y = x_y.transpose(0, 2, 1)[:, :, None, :]
        x_y = jax.nn.sigmoid(x_y + a_w)
        x_y = _c1x1(gelu(_c1x1(x_y, mlpy_w1, mlpy_b1)), mlpy_w2, mlpy_b2)
        result_h = jax.nn.sigmoid(a_h) * x_y
        result_w = jax.nn.sigmoid(a_w) * x_x
        out1 = _c1x1(jnp.concatenate([result_h, result_w], axis=1), adjust_w)
        return x * out1

    def _L3_conv_ref(x, pre_w, pre_b, q_weights, post_w, post_b):
        import jax, jax.numpy as jnp
        import numpy as np
        NQ = 4
        NL = 2

        def _apply_1q(state, U, w):
            state = jnp.moveaxis(state, w + 1, -1)
            state = jnp.einsum('ij,...j->...i', U, state)
            return jnp.moveaxis(state, -1, w + 1)

        def _apply_cnot(state, cw, tw):
            s0 = jnp.take(state, jnp.array([0]), axis=cw + 1)
            s1 = jnp.take(state, jnp.array([1]), axis=cw + 1)
            s1 = jnp.flip(s1, axis=tw + 1)
            return jnp.concatenate([s0, s1], axis=cw + 1)

        def _simulate(xq, qw):
            half = 0.5 * jnp.pi * xq
            c, s = (jnp.cos(half), jnp.sin(half))
            state = jnp.stack([c[:, 0], s[:, 0]], axis=-1).astype(jnp.complex64)
            for w in range(1, NQ):
                q = jnp.stack([c[:, w], s[:, w]], axis=-1).astype(jnp.complex64)
                state = jnp.einsum('b...,bj->b...j', state, q)
            for l in range(NL):
                for w in range(NQ):
                    phi, theta, omega = (qw[l, w, 0], qw[l, w, 1], qw[l, w, 2])
                    ct = jnp.cos(0.5 * theta)
                    st = jnp.sin(0.5 * theta)
                    a = 0.5 * (phi + omega)
                    b = 0.5 * (phi - omega)
                    row0 = jnp.stack([jnp.exp(-1j * a) * ct, -jnp.exp(1j * b) * st])
                    row1 = jnp.stack([jnp.exp(-1j * b) * st, jnp.exp(1j * a) * ct])
                    U = jnp.stack([row0, row1]).astype(jnp.complex64)
                    state = _apply_1q(state, U, w)
                r = l % (NQ - 1) + 1
                for w in range(NQ):
                    state = _apply_cnot(state, w, (w + r) % NQ)
            p = state.real ** 2 + state.imag ** 2
            ez = []
            for w in range(NQ):
                axes = tuple((a for a in range(1, NQ + 1) if a != w + 1))
                m = p.sum(axis=axes)
                ez.append(m[:, 0] - m[:, 1])
            return jnp.stack(ez, axis=1)
        N, C, H, W = x.shape
        xf = x.transpose(0, 2, 3, 1).reshape(-1, C)
        xq = xf @ pre_w.T + pre_b
        z = _simulate(xq, q_weights)
        out = z @ post_w.T + post_b
        return out.reshape(N, H, W, -1).transpose(0, 3, 1, 2)

    def _gn(v, G=32, eps=1e-5):
        B_, C_, H_, W_ = v.shape
        g = v.reshape(B_, G, C_ // G, H_, W_)
        m = jnp.mean(g, axis=(2, 3, 4), keepdims=True)
        s = jnp.var(g, axis=(2, 3, 4), keepdims=True)
        return ((g - m) / jnp.sqrt(s + eps)).reshape(v.shape)

    def _ln_c(v, eps=1e-6):
        m = jnp.mean(v, axis=1, keepdims=True)
        s = jnp.var(v, axis=1, keepdims=True)
        return (v - m) / jnp.sqrt(s + eps)

    def _ln_t(v, eps=1e-5):
        m = jnp.mean(v, axis=-1, keepdims=True)
        s = jnp.var(v, axis=-1, keepdims=True)
        return (v - m) / jnp.sqrt(s + eps)

    def _to_tokens(v):
        B_, C_, H_, W_ = v.shape
        return v.reshape(B_, C_, H_ * W_).transpose(0, 2, 1)
    def _from_tokens(t, like):
        B_, C_, H_, W_ = like.shape
        return t.transpose(0, 2, 1).reshape(B_, C_, H_, W_)

    x = x + _L0_conv_ref(_gn(x), L0_conv_weight, L0_conv_bias)
    x = x + _L1_conv_ref(_gn(x), L1_conv_nin_w, L1_conv_bn1_g, L1_conv_bn1_b, L1_conv_bn1_m, L1_conv_bn1_v, L1_conv_in_proj_w, L1_conv_conv_w, L1_conv_conv_b, L1_conv_x_proj_w, L1_conv_dt_proj_w, L1_conv_dt_proj_b, L1_conv_A_log, L1_conv_D, L1_conv_out_proj_w, L1_conv_nin2_w, L1_conv_bn2_g, L1_conv_bn2_b, L1_conv_bn2_m, L1_conv_bn2_v)
    x = x + _L2_conv_ref(_gn(x), L2_conv_conv1_w, L2_conv_conv1_b, L2_conv_bn_g, L2_conv_bn_b, L2_conv_bn_m, L2_conv_bn_v, L2_conv_convh_w, L2_conv_convh_b, L2_conv_convw_w, L2_conv_convw_b, L2_conv_mlpx_w1, L2_conv_mlpx_b1, L2_conv_mlpx_w2, L2_conv_mlpx_b2, L2_conv_mlpy_w1, L2_conv_mlpy_b1, L2_conv_mlpy_w2, L2_conv_mlpy_b2, L2_conv_adjust_w, L2_conv_mx_in_w, L2_conv_mx_conv_w, L2_conv_mx_conv_b, L2_conv_mx_xproj_w, L2_conv_mx_dt_w, L2_conv_mx_dt_b, L2_conv_mx_Alog, L2_conv_mx_D, L2_conv_mx_out_w, L2_conv_my_in_w, L2_conv_my_conv_w, L2_conv_my_conv_b, L2_conv_my_xproj_w, L2_conv_my_dt_w, L2_conv_my_dt_b, L2_conv_my_Alog, L2_conv_my_D, L2_conv_my_out_w)
    x = x + _L3_conv_ref(_gn(x), L3_conv_pre_w, L3_conv_pre_b, L3_conv_q_weights, L3_conv_post_w, L3_conv_post_b)
    return x


_drawn_inputs = setup_inputs


def setup_inputs(seed=0):
    import zlib

    import numpy as np

    out = dict(_drawn_inputs(seed))
    spreads = {'L1_conv_bn1_g': (1.0, 0.2),
     'L1_conv_bn1_b': (0.0, 0.1),
     'L1_conv_bn1_m': (0.0, 0.1),
     'L1_conv_bn1_v': (1.0, 0.2),
     'L1_conv_conv_b': (0.0, 0.1),
     'L1_conv_D': (1.0, 0.2),
     'L1_conv_bn2_g': (1.0, 0.2),
     'L1_conv_bn2_b': (0.0, 0.1),
     'L1_conv_bn2_m': (0.0, 0.1),
     'L1_conv_bn2_v': (1.0, 0.2),
     'L2_conv_bn_g': (1.0, 0.2),
     'L2_conv_bn_b': (0.0, 0.1),
     'L2_conv_bn_m': (0.0, 0.1),
     'L2_conv_bn_v': (1.0, 0.2),
     'L2_conv_mx_D': (1.0, 0.2),
     'L2_conv_my_D': (1.0, 0.2)}
    factors = {}
    for name, (base, spread) in spreads.items():
        noise = np.random.default_rng([zlib.crc32(name.encode()), seed]).standard_normal(out[name].shape)
        drawn = base * np.exp(spread * noise) if base else spread * noise
        out[name] = jnp.asarray(drawn.astype(out[name].dtype))
    for name, factor in factors.items():
        out[name] = (out[name] * factor).astype(out[name].dtype)
    return out
```

```python
from contextlib import ExitStack

import numpy as np
import concourse.bass as bass
from concourse import mybir

F32 = mybir.dt.float32
BF16 = mybir.dt.bfloat16
ALU = mybir.AluOpType
ACT = mybir.ActivationFunctionType
AX = mybir.AxisListType

IMAGES, P, SIDE = 32, 128, 32
TOK = SIDE * SIDE
BANK = 512
HALVES = 2
DI = HALVES * P
NST = 16
RANK = 8
TAPS = 4
PAD = TAPS - 1
DIRS = 4
PASSES = DIRS * HALVES
UNITS = PASSES * NST
RING = 4
BRING = 2
XP = 3 * 2 * NST + RANK
DTP = 3 * 2 * NST
XP2 = RANK + 2 * NST
MH = 4
NQ = 4
GATES = 2 * NQ
AMPS = 2 ** NQ
CH = TOK // P
GROUP = 4
PI = float(np.pi)
TWO_PI = 6.283185
ROUND = 1.5 * 2 ** 23

KEEP = [
    ("conv0", 9 * P), ("nin", P), ("z", 2 * DI), ("xproj", HALVES * XP), ("nin2", P), ("ident", P),
    ("gavg", P), ("alog", HALVES * NST), ("conv0_b", 1), ("conv_b", HALVES), ("dt_b", HALVES),
    ("D", HALVES), ("bn1", 4), ("bn2", 4), ("squeeze", 8), ("mlp1x", P), ("mlp1y", P), ("mlp2x", P),
    ("mlp2y", P), ("adjust", 2 * P), ("in2", 2 * 2 * DI), ("taps2", MH * TAPS), ("conv2_b", MH),
    ("xproj2", MH * XP2), ("dt2_b", MH), ("alog2", MH * NST), ("D2", MH), ("out2", MH * P),
    ("gate_b", 2), ("mlp1_b", 2), ("mlp2_b", 2), ("pre", NQ), ("post_b", 1), ("negstack", 96),
    ("rowmask", CH),
]
ONCE = [("in", 2 * DI), ("outp", 2 * DI), ("perm1", AMPS), ("perm2", AMPS), ("rep", P), ("sign", P),
        ("post", P)]
SMALL = [("spread_h", P), ("spread_w", P), ("dtp2", 2 * DI), ("bn", 4), ("squeeze_b", 1)]


def columns(table):
    at, out = 0, {}
    for name, width in table:
        out[name] = (at, at + width)
        at += width
    return out, at


def circuit_entangler(layer):
    r = layer % (NQ - 1) + 1
    to = list(range(AMPS))
    for w in range(NQ):
        c, t = NQ - 1 - w, NQ - 1 - (w + r) % NQ
        to = [k ^ (1 << t) if k >> c & 1 else k for k in to]
    return to


def norm(tag):
    return [(("stats", tag, 0), "D"), (("stats", tag, 1), "D"), (("square", tag), "D"),
            (("mean_square", tag), "D"), (("group_mean", tag), "P"), (("group_copy", tag), "D"),
            (("group_negvar", tag), "D"), (("group_eps", tag), "D"), (("group_rstd", tag), "G"),
            (("group_shift", tag), "D"), (("norm", tag), "D")]


def front():
    return (norm("0") + [(("conv0", k), "P") for k in range(9)] + [(("add0",), "D")] + norm("1")
            + [(("nin",), "P"), (("h1",), "A")])


def operands(d):
    steps = []
    for h in range(HALVES):
        steps += [(("conv_in", d, h, k), "P") for k in range(TAPS)] + [(("silu_u", d, h), "A")]
    if d % 2:
        for h in range(HALVES):
            steps += [(("z", d, h), "P"), (("silu_z", d, h), "A")]
    steps += [(("xproj", d, c), "P") for c in range(2)] + [(("dt_rows", d), "A")]
    steps += [(("part", d, 0), "A"), (("rest", d, 0), "P"), (("part", d, 1), "A"),
              (("rest", d, 1), "P"), (("part", d, 2), "A")]
    return steps


def timestep(d, h):
    return [(("dt_proj", d, h), "P"), (("dt_abs", d, h), "A"), (("dt_relu", d, h), "A"),
            (("dt_exp", d, h), "A"), (("dt_ln", d, h), "A"), (("dt_sum", d, h), "D"),
            (("dt_u", d, h), "D")]


def spread_c(d, n):
    return [(("c_spread", d, n), "P"), (("c_copy", d, n), "A")]


def mix():
    return [(("mix", k), "P") for k in range(5)]


def back():
    s = [(("relu2",), "A"), (("add1",), "D")] + norm("2")
    s += [((k,), "D") for k in ("rows", "cols", "means")]
    s += [(("squeeze",), "P"), (("squeeze_gelu",), "A"), (("gates",), "P"), (("gate_h",), "D"),
          (("gate_w",), "D"), (("gate_tanh",), "A"), (("gate_sig",), "D"), (("in2",), "P"),
          (("pad2",), "D"), (("z2",), "D"), (("taps2",), "D"), (("tapsum2",), "D"),
          (("tapbias2",), "D"), (("silu2",), "A"), (("xproj2",), "P"), (("xcopy2",), "D"),
          (("dtproj2",), "P"), (("dtbias2",), "D"), (("dtabs2",), "A"), (("dtrelu2",), "A"),
          (("dtexp2",), "A"), (("dtln2",), "A"), (("dtsum2",), "D"), (("du2",), "D")]
    for m in range(2):
        s += [(("spread2", m, q), "P") for q in range(4)]
        for h in range(HALVES):
            s += [(("dta2", m, h), "D"), (("decay2", m, h), "A"), (("start2", m, h), "D"),
                  (("input2", m, h), "D"), (("scan2", m, h), "D"), (("prod2", m, h), "D"),
                  (("ysum2", m, h), "D")]
    s += [(("dterm2",), "D"), (("dadd2",), "D"), (("yz2",), "D"), (("out2",), "P"), (("xa",), "D"),
          (("xa_tanh",), "A"), (("xa_sig",), "D"), (("mlp1",), "P"), (("mlp_gelu", 0), "A"),
          (("mlp_gelu", 1), "A"), (("mlp2",), "P"), (("mlp_b", 0), "D"), (("mlp_b", 1), "D"),
          (("outer_h",), "D"), (("outer_w",), "D"), (("adjust", 0), "P"), (("adjust", 1), "P"),
          (("times_x",), "D"), (("add2",), "D")] + norm("3")
    s += [(("angles",), "P"), (("angle_b",), "D"), (("turns", 1), "D"), (("turns", 0), "D"),
          (("round_up",), "D"), (("round_down",), "D"), (("fraction",), "D"), (("sine",), "A"),
          (("pair", 0), "D"), (("pair", 1), "D"), (("amplitudes",), "D"), (("turn",), "P"),
          (("turn_copy",), "D"), (("unitary",), "P"), (("probability",), "A"), (("post", 0), "P"),
          (("post", 1), "P"), (("result",), "D")]
    return s


def setup():
    s = [(("zero",), "G"), (("small_bf16",), "D"), (("halfs",), "D")]
    s += [(("fuse", f, k), "D") for f in range(2) for k in range(TAPS)]
    s += [(("diag", h), "D") for h in range(HALVES)]
    s += [(("a_exp",), "A"), (("a_exp2",), "A"), (("a_neg",), "D"), (("a_neg2",), "D")]
    for b in ("bn1", "bn2", "bn"):
        s += [(("bn_eps", b), "D"), (("bn_rstd", b), "G"), (("bn_scale", b), "D"), (("bn_ms", b), "D"),
              (("bn_shift", b), "D")]
    s += [(("bn_bias",), "D"), (("bn_bias2",), "D"), (("preb",), "D")]
    for f in range(2):
        for h in range(HALVES):
            s += [(("mixw", f, h), "P"), (("mixw_copy", f, h), "D")]
    s += [((k,), "D") for k in ("q_sum", "q_diff", "q_quarter", "q_up", "q_down", "q_frac")]
    s += [(("q_sin",), "A")]
    s += [(("gate", k), "D") for k in range(8)] + [(("gate_negs",), "D")]
    for n in range(3):
        s += [(("kron", n, 0), "D"), (("kron", n, 1), "D"), (("kron", n, 2), "D")]
    return s


def setup2():
    s = [(("m1",), "P"), (("m1_copy",), "D"), (("q_neg",), "D"), (("tt",), "P"), (("tt_copy",), "D"), (("blocks",), "P"), (("blocks_mask", 0), "D"),
         (("blocks_mask", 1), "D"), (("postw",), "P")]
    s += [(("postw_mask", j), "D") for j in range(CH)]
    return s


def place(steps, slot0, slots):
    n = len(steps)
    return [(slot0 + i * slots // n, name, e) for i, (name, e) in enumerate(steps)]


def image_plan(first, last):
    plan = []
    rest = [] if first else back()
    share = [rest[:len(rest) // 3], rest[len(rest) // 3:2 * len(rest) // 3], rest[2 * len(rest) // 3:]]
    for d in range(DIRS):
        at = 2 * d * NST
        work = timestep(d, 1)
        if d == 0 and not first:
            work = work + mix()
        more = d < DIRS - 1 or not last
        nxt = (d + 1) % DIRS
        if d < 3:
            work = work + share[d]
        elif not last:
            work = work + front()
        if more:
            work = work + operands(nxt)
        early = 2 if d else 0
        plan += place(work, at + early, NST - early)
        at += NST
        if more:
            plan += place(timestep(nxt, 0), at, 4)
            for n in range(NST):
                plan += [(at + max(n + 2, 4), name, e) for name, e in spread_c(nxt, n)]
    for i in range(1, len(plan)):
        if plan[i][0] < plan[i - 1][0]:
            plan[i] = (plan[i - 1][0], *plan[i][1:])
    return [(min(slot, UNITS), name, e) for slot, name, e in plan]


def four_layers(nc, images, x_in, keep, once, small, dtw, conv_wt, preb_row, qw, out):
    KC, keep_w = columns(KEEP)
    OC, once_w = columns(ONCE)
    SC, small_w = columns(SMALL)
    lead = setup()
    lead2 = setup2()
    begin = front() + operands(0) + timestep(0, 0)
    for n in range(NST):
        begin = begin + spread_c(0, n)
    plans = {"first": image_plan(True, images == 1), "mid": image_plan(False, False),
             "last": image_plan(False, True)}
    finish = mix() + back()
    lead2_at = len(lead)
    begin_at = lead2_at + len(lead2)
    first_at = begin_at + len(begin)
    mid_len = len(plans["mid"])
    image1_at = first_at + len(plans["first"])

    def start_of(kind, s):
        return first_at if kind == "first" else image1_at + (s - 1) * mid_len

    def pos_in(kind, name):
        return [x[1] for x in plans[kind]].index(name)

    def end_of_back(kind):
        return pos_in(kind, ("result",)) + 1

    with ExitStack() as ctx:
        def sb(name, shape, dt=F32):
            return ctx.enter_context(nc.sbuf_tensor(name, shape, dt))

        def sem(name):
            return ctx.enter_context(nc.semaphore(name))

        c_all = sb("c_all", [P, NST, TOK])
        u_conv = sb("u_conv", [P, 2, HALVES, TOK])
        dt = sb("dt", [P, HALVES, TOK])
        du = sb("du", [P, HALVES, TOK])
        ring = sb("ring", [P, RING, TOK])
        silu_z = sb("silu_z", [P, HALVES, TOK])
        yz = sb("yz", [P, 2, HALVES, TOK])
        x_new = sb("x_new", [P, TOK])
        x_old = sb("x_old", [P, TOK])
        h_new = sb("h_new", [P, TOK + 2 * PAD])
        h_old = sb("h_old", [P, TOK])
        padded = sb("padded", [P, SIDE + 2, SIDE + 2])
        stack = sb("stack", [P, 2, TOK], BF16)
        wk = sb("wk", [P, keep_w])
        smallw = sb("smallw", [P, small_w])
        fused = sb("fused", [P, 2, TAPS, DI])
        diag_d = sb("diag_d", [P, HALVES, P])
        mixw = sb("mixw", [P, 2, HALVES, P])
        unitary = sb("unitary", [P, 2, P])
        postw = sb("postw", [P, CH, P])
        a_neg = sb("a_neg", [P, HALVES * NST])
        a_neg2 = sb("a_neg2", [P, MH * NST])
        sel = sb("sel", [P, 96], BF16)
        negsel = sb("negsel", [P, 96], BF16)
        preb = sb("preb", [P, NQ])
        neghalf = sb("neghalf", [P, 1])
        bnw = sb("bnw", [P, 3, 8])
        gn = sb("gn", [P, 32])
        s64 = sb("s64", [P, 8, 64])
        m128 = sb("m128", [P, 6, 128])
        upad = sb("upad", [P, MH, SIDE + PAD])
        g8 = sb("g8", [RANK, 64])
        dbl = sb("dbl", [XP2, 64])
        circ = sb("circ", [P, 2, CH, NQ])
        circq = sb("circq", [P, 2, CH, NQ])

        dt_rows = stack[:, :, :].rearrange("p a t -> p (a t)").bitcast(F32)[DTP:DTP + RANK, :]
        dtw_sb = smallw[:, 0:DI]
        bring = ctx.enter_context(nc.psum_tensor("bring", [P, BRING, TOK], F32))
        y_acc = ctx.enter_context(nc.psum_tensor("y_acc", [P, TOK], F32))
        work = ctx.enter_context(nc.psum_tensor("work", [P, TOK], F32))

        side = sem("side")
        weights_in = sem("weights_in")
        b_ready = sem("b_ready")
        decay_ready = sem("decay_ready")
        input_ready = sem("input_ready")
        scan_done = sem("scan_done")
        prod_ready = sem("prod_ready")
        sum_done = sem("sum_done")
        y_taken = sem("y_taken")
        x_loaded = sem("x_loaded")
        old_kept = sem("old_kept")
        out_stored = sem("out_stored")
        matrices_in = sem("matrices_in")

        def kc(name, a=0, b=None):
            lo, hi = KC[name]
            return wk[:, lo + a:(hi if b is None else lo + b)]

        def s8(name, a=0, b=None):
            lo, hi = SC[name]
            return smallw[0:RANK, lo + a:(hi if b is None else lo + b)]

        scratch = c_all[:, :, :].rearrange("p n t -> p (n t)")
        once_sb = scratch[:, 0:once_w]
        conv_rows = scratch[:, 2048:2048 + TAPS * DI]
        q_sb = scratch[0:1, 3072:3072 + 16 * GATES]
        turns, turns_whole = q_sb[:, 48:96], scratch[0:1, 3408:3408 + 48]
        sines = scratch[0:1, 4608:4608 + 48]
        gate_m = scratch[0:1, 3200:3200 + 3 * 4 * GATES]
        kr01 = scratch[0:1, 3328:3328 + 3 * 2 * AMPS]
        kr23 = scratch[0:1, 3456:3456 + 3 * 2 * AMPS]
        kr = scratch[0:1, 3584:3584 + 2 * 2 * AMPS * AMPS]
        krt = scratch[0:1, 4608:4608 + 512]
        lay = scratch[0:AMPS, 5120:5120 + 5 * AMPS]
        m1 = scratch[0:AMPS, 5248:5248 + 4 * AMPS]
        q_neg = scratch[0:AMPS, 5312:5312 + AMPS]
        ttc = scratch[0:AMPS, 5376:5376 + 2 * AMPS]
        sb_t = scratch[:, 5504:5504 + P]

        def oc(name, a=0, b=None, rows=P):
            lo, hi = OC[name]
            return once_sb[0:rows, lo + a:(hi if b is None else lo + b)]

        t0 = yz[:, 1, 0, :]
        t1 = yz[:, 1, 1, :]
        inner = padded[:, 1:SIDE + 1, 1:SIDE + 1]
        h_mid = h_new[:, PAD:PAD + TOK]
        tile2d = lambda ap: ap.rearrange("p (a b) -> p a b", b=SIDE)
        NORM = {"0": (x_new[:, :], tile2d(x_new[:, :]), inner), "1": (x_new[:, :], x_new[:, :], h_mid),
                "2": (x_old[:, :], x_old[:, :], t0), "3": (x_old[:, :], x_old[:, :], t0)}

        gate_a, gate_s, xa, ml, xxy, um = (s64[:, i, :] for i in range(6))
        u2, z2, dt2, du2, sp2, yy2 = (m128[:, i, :] for i in range(6))
        mh = lambda ap: ap.rearrange("p (m t) -> p m t", m=MH)
        per_mh = lambda ap: ap.unsqueeze(2).broadcast_to([P, MH, SIDE])

        block = ctx.enter_context(nc.Block())

        def unit_of(u):
            return u // (2 * NST), u // NST % HALVES, u % NST

        def each_image(eng, body):
            body("first", 0)
            if images > 2:
                with eng.Fori(1, images - 1) as s:
                    body("mid", s)
            if images > 1:
                body("last", images - 1)

        def late(name):
            return name

        @block.sync
        def _(sp):
            sp.dma_start(wk[:, :], keep).then_inc(weights_in, 16)
            sp.dma_start(once_sb, once).then_inc(weights_in, 16)
            sp.dma_start(smallw[0:RANK, :], small).then_inc(weights_in, 16)
            sp.dma_start(dtw_sb[DTP:DTP + RANK, :], dtw).then_inc(weights_in, 16)
            sp.dma_start(conv_rows, conv_wt.partition_broadcast(P)).then_inc(weights_in, 16)
            sp.dma_start(preb[:, :], preb_row.partition_broadcast(P)).then_inc(weights_in, 16)
            sp.dma_start(q_sb[:, 0:3 * GATES], qw).then_inc(weights_in, 16)
            sp.dma_start(x_new[:, :], x_in[0]).then_inc(x_loaded, 16)
            sp.wait_ge(side, lead2_at)
            for c in range(2):
                k1 = kr[:, c * 512:c * 512 + 256].rearrange("p (a b) -> p a b", b=AMPS)
                k2 = kr[:, c * 512 + 256:c * 512 + 512].rearrange("p (a b) -> p a b", b=AMPS)
                sp.dma_start(lay[:, c * AMPS:(c + 1) * AMPS], k1).then_inc(matrices_in, 16)
                sp.dma_start(lay[:, (2 + c) * AMPS:(3 + c) * AMPS], k2).then_inc(matrices_in, 16)

            def image(kind, s):
                base = start_of(kind, s)
                if kind != "first":
                    sp.wait_ge(side, base + end_of_back(kind))
                    sp.dma_start(out[s - 1], t0).then_inc(out_stored, 16)
                if kind != "last":
                    sp.wait_ge(side, base + (0 if kind == "first" else end_of_back(kind)))
                    sp.dma_start(x_old[:, :], x_new[:, :]).then_inc(old_kept, 16)
                    sp.dma_start(h_old[:, :], h_mid).then_inc(old_kept, 16)
                    sp.wait_ge(old_kept, 32 * s + 32)
                    sp.dma_start(x_new[:, :], x_in[s + 1]).then_inc(x_loaded, 16)
                else:
                    sp.wait_ge(side, base + end_of_back(kind))
                    sp.dma_start(x_old[:, :], x_new[:, :]).then_inc(old_kept, 16)
                    sp.dma_start(h_old[:, :], h_mid).then_inc(old_kept, 16)

            each_image(sp, image)
            sp.wait_ge(side, start_of("last", images - 1) + len(plans["last"]) + len(finish))
            sp.dma_start(out[images - 1], t0).then_inc(out_stored, 16)
            sp.wait_ge(out_stored, 16 * images)

        @block.gpsimd
        def _(pool):
            def step(name, pos, s):
                if not (isinstance(pos, int) and pos == 0):
                    pool.wait_ge(side, pos)
                k = name[0]
                if k == "zero":
                    pool.memset(padded[:, :, :], 0.0)
                    pool.memset(upad[:, :, :], 0.0)
                    pool.memset(neghalf[:, :], -0.5)
                    ins = pool.memset(h_new[:, :], 0.0)
                elif k == "bn_rstd":
                    r, b = (RANK, 2) if name[1] == "bn" else (P, ("bn1", "bn2").index(name[1]))
                    ins = pool.tensor_tensor(bnw[0:r, b, 1:2], bnw[0:r, b, 0:1], neghalf[0:r, :], ALU.pow)
                elif k == "group_rstd":
                    ins = pool.tensor_tensor(gn[:, 19:20], gn[:, 18:19], neghalf[:, :], ALU.pow)
                ins.then_inc(side, 1)

            def walk(steps, at, s):
                for i, (name, e) in enumerate(steps):
                    if e == "G":
                        step(name, at + i, s)

            walk(lead + lead2 + begin, 0, 0)

            def image(kind, s):
                plan, base = plans[kind], start_of(kind, s)
                names = [x[1] for x in plan]
                for u in range(UNITS + 1):
                    if u < UNITS:
                        d, h, n = unit_of(u)
                        if h == 0 and d > 0:
                            pool.wait_ge(side, base + names.index(("c_copy", d, n)) + 1)
                        elif u == 0:
                            pool.wait_ge(side, base)
                        pool.wait_ge(scan_done, s * UNITS + u + 1)
                        slot = ring[:, u % RING, :]
                        pool.tensor_tensor(slot, slot, c_all[:, n, :], ALU.mult).then_inc(prod_ready, 1)
                    for i, (at, name, e) in enumerate(plan):
                        if at == u and e == "G":
                            step(name, base + i, s)

            each_image(pool, image)
            walk(finish, start_of("last", images - 1) + len(plans["last"]), images - 1)

        @block.scalar
        def _(act):
            def step(name, pos, s):
                act.wait_ge(side, pos)
                k = name[0]
                if k == "a_exp":
                    ins = act.activation(a_neg[:, :], kc("alog"), ACT.Exp)
                elif k == "a_exp2":
                    ins = act.activation(a_neg2[:, :], kc("alog2"), ACT.Exp)
                elif k == "q_sin":
                    ins = act.activation(sines, turns, ACT.Sin, scale=TWO_PI)
                elif k == "h1":
                    if not (isinstance(s, int) and s == 0):
                        act.wait_ge(old_kept, 32 * s)
                    ins = act.activation(h_mid, work[:, :], ACT.Relu, bias=bnw[:, 0, 4:5],
                                         scale=bnw[:, 0, 2:3])
                elif k == "silu_u":
                    _, d, h = name
                    ins = act.activation(u_conv[:, d % 2, h, :], work[:, :], ACT.Silu,
                                         bias=kc("conv_b", h, h + 1))
                elif k == "silu_z":
                    if not (isinstance(s, int) and s == 0 and name[1] == 1):
                        act.wait_ge(y_taken, s * PASSES + name[1] // 2 * 4)
                    ins = act.activation(silu_z[:, name[2], :], work[:, :], ACT.Silu)
                elif k == "dt_rows":
                    ins = act.activation(dt_rows, work[DTP:DTP + RANK, :], ACT.Copy)
                elif k == "part":
                    _, d, i = name
                    r = slice(32 * i, 32 * i + 32)
                    ins = act.activation(stack[r, d % 2, :], work[r, :], ACT.Copy)
                elif k == "dt_abs":
                    _, d, h = name
                    done = d * 2 * NST + (h - 1) * NST
                    if d or h:
                        act.wait_ge(input_ready, s * UNITS + done)
                    elif not (isinstance(s, int) and s == 0):
                        act.wait_ge(input_ready, s * UNITS + done)
                    if isinstance(s, int) and s * UNITS + done <= 0:
                        pass
                    else:
                        act.wait_ge(decay_ready, s * UNITS + done)
                    ins = act.activation(du[:, h, :], work[:, :], ACT.Abs, bias=kc("dt_b", h, h + 1))
                elif k == "dt_relu":
                    h = name[2]
                    ins = act.activation(dt[:, h, :], work[:, :], ACT.Relu, bias=kc("dt_b", h, h + 1))
                elif k == "dt_exp":
                    h = name[2]
                    ins = act.activation(du[:, h, :], du[:, h, :], ACT.Exp, scale=-1.0)
                elif k == "dt_ln":
                    h = name[2]
                    ins = act.activation(du[:, h, :], du[:, h, :], ACT.Ln, bias=1.0)
                elif k == "c_copy":
                    _, d, n = name
                    last = (d - 1) * 2 * NST + NST + n + 1
                    if d or not (isinstance(s, int) and s == 0):
                        act.wait_ge(prod_ready, s * UNITS + last)
                    ins = act.activation(c_all[:, n, :], work[:, :], ACT.Copy)
                elif k == "relu2":
                    ins = act.activation(t0, work[:, :], ACT.Relu, bias=bnw[:, 1, 4:5],
                                         scale=bnw[:, 1, 2:3])
                elif k == "squeeze_gelu":
                    ins = act.activation(g8[:, :], work[0:RANK, 0:64], ACT.Gelu, bias=bnw[0:RANK, 2, 5:6],
                                         scale=bnw[0:RANK, 2, 2:3])
                elif k == "gate_tanh":
                    ins = act.activation(gate_s, gate_a, ACT.Tanh, scale=0.5)
                elif k == "silu2":
                    act.activation(u2, u2, ACT.Silu)
                    ins = act.activation(z2, z2, ACT.Silu)
                elif k == "dtabs2":
                    ins = act.activation(sp2, dt2, ACT.Abs)
                elif k == "dtrelu2":
                    ins = act.activation(dt2, dt2, ACT.Relu)
                elif k == "dtexp2":
                    ins = act.activation(sp2, sp2, ACT.Exp, scale=-1.0)
                elif k == "dtln2":
                    ins = act.activation(sp2, sp2, ACT.Ln, bias=1.0)
                elif k == "decay2":
                    ins = act.activation(t1[:, 0:512], t1[:, 0:512], ACT.Exp)
                elif k == "xa_tanh":
                    ins = act.activation(xa, xa, ACT.Tanh, scale=0.5)
                elif k == "mlp_gelu":
                    m = name[1]
                    ins = act.activation(ml[:, 32 * m:32 * m + 32], work[:, 32 * m:32 * m + 32], ACT.Gelu,
                                         bias=kc("mlp1_b", m, m + 1))
                elif k == "sine":
                    ins = act.activation(circ[:, :, :, :].rearrange("p a j w -> p (a j w)"),
                                         circq[:, :, :, :].rearrange("p a j w -> p (a j w)"), ACT.Sin,
                                         scale=TWO_PI)
                elif k == "probability":
                    ins = act.activation(t0[:, 0:256], work[:, 0:256], ACT.Square)
                ins.then_inc(side, 1)

            def walk(steps, at, s):
                for i, (name, e) in enumerate(steps):
                    if e == "A":
                        step(name, at + i, s)

            walk(lead + lead2 + begin, 0, 0)

            def image(kind, s):
                plan, base = plans[kind], start_of(kind, s)
                names = [x[1] for x in plan]

                def decay(u):
                    d, h, n = unit_of(u)
                    if n == 0:
                        act.wait_ge(side, base + (names.index(("dt_sum", d, h)) + 1 if u else 0))
                    if u >= RING or not (isinstance(s, int) and s == 0):
                        act.wait_ge(sum_done, s * UNITS + u - RING + 1)
                    act.activation(ring[:, u % RING, :], dt[:, h, :], ACT.Exp,
                                   scale=a_neg[:, h * NST + n:h * NST + n + 1]).then_inc(decay_ready, 1)

                def take_y(p):
                    f, t, h = p // 4, p // 2 % 2, p % 2
                    if t == 0:
                        act.wait_ge(sum_done, s * UNITS + (p + 1) * NST)
                        if kind != "first":
                            act.wait_ge(side, base + (end_of_back(kind) if f else
                                                      names.index(("mix", 4)) + 1))
                            if f:
                                act.wait_ge(out_stored, 16 * s)
                        act.activation(yz[:, f, h, :], y_acc[:, :], ACT.Copy).then_inc(y_taken, 1)

                decay(0)
                for u in range(UNITS + 1):
                    if u + 1 < UNITS:
                        decay(u + 1)
                    if u % NST == 2 and u > 2:
                        take_y(u // NST - 1)
                    for i, (at, name, e) in enumerate(plan):
                        if at == u and e == "A":
                            nxt = name[0] in ("h1",) or (len(name) > 1 and name[1] == 0
                                                         and name[0] in ("silu_u", "dt_rows", "part", "c_copy")
                                                         or name[0][:3] == "dt_" and name[1:] == (0, 0))
                            step(name, base + i, s + 1 if nxt else s)
            each_image(act, image)
            walk(finish, start_of("last", images - 1) + len(plans["last"]), images - 1)

        @block.vector
        def _(dve):
            MUL, ADD, SUB = ALU.mult, ALU.add, ALU.subtract
            stat = gn[:, 0:12].rearrange("p (i c) -> p i c", c=3)

            def step(name, pos, s):
                dve.wait_ge(side, pos)
                k = name[0]
                if k == "small_bf16":
                    dve.tensor_copy(negsel[0:96, :], kc("negstack")[0:96, :])
                    ins = dve.tensor_scalar(sel[0:96, :], kc("negstack")[0:96, :], -1.0, None, MUL)
                elif k == "halfs":
                    ins = dve.tensor_scalar(preb[:, :], preb[:, :], 1.0, None, MUL)
                elif k == "fuse":
                    _, f, j = name
                    ins = dve.tensor_tensor(fused[:, f, j, :], oc("in", f * DI, (f + 1) * DI),
                                            conv_rows[:, j * DI:(j + 1) * DI], MUL)
                elif k == "diag":
                    h = name[1]
                    ins = dve.tensor_scalar(diag_d[:, h, :], kc("ident"), kc("D", h, h + 1), None, MUL)
                elif k == "a_neg":
                    ins = dve.tensor_scalar(a_neg[:, :], a_neg[:, :], -1.0, None, MUL)
                elif k == "a_neg2":
                    ins = dve.tensor_scalar(a_neg2[:, :], a_neg2[:, :], -1.0, None, MUL)
                elif k[:3] == "bn_" and len(name) > 1:
                    b = ("bn1", "bn2", "bn").index(name[1])
                    r = RANK if b == 2 else P
                    g = (lambda i: s8("bn", i, i + 1)) if b == 2 else (lambda i: kc(name[1], i, i + 1))
                    w = bnw[0:r, b, :]
                    if k == "bn_eps":
                        ins = dve.tensor_scalar(w[:, 0:1], g(3), 1e-5, None, ADD)
                    elif k == "bn_scale":
                        ins = dve.tensor_tensor(w[:, 2:3], w[:, 1:2], g(0), MUL)
                    elif k == "bn_ms":
                        ins = dve.tensor_tensor(w[:, 3:4], w[:, 2:3], g(2), MUL)
                    else:
                        ins = dve.tensor_tensor(w[:, 4:5], g(1), w[:, 3:4], SUB)
                elif k == "bn_bias":
                    ins = dve.tensor_tensor(bnw[0:RANK, 2, 6:7], bnw[0:RANK, 2, 2:3], s8("squeeze_b"), MUL)
                elif k == "bn_bias2":
                    ins = dve.tensor_tensor(bnw[0:RANK, 2, 5:6], bnw[0:RANK, 2, 4:5], bnw[0:RANK, 2, 6:7], ADD)
                elif k == "preb":
                    ins = dve.tensor_scalar(preb[:, :], preb[:, :], 1.0, None, MUL)
                elif k == "mixw_copy":
                    _, f, h = name
                    ins = dve.tensor_scalar(mixw[:, f, h, :], work[:, 0:P], 0.25, None, MUL)
                elif k == "q_sum":
                    ins = dve.tensor_tensor(q_tmp(0), angle(0), angle(2), ADD)
                elif k == "q_diff":
                    ins = dve.tensor_tensor(q_tmp(1), angle(0), angle(2), SUB)
                elif k == "q_quarter":
                    dve.tensor_scalar(qt(0, 0), angle(1), 0.5 / (2 * PI), None, MUL)
                    dve.tensor_scalar(qt(0, 1), angle(1), 0.5 / (2 * PI), 0.25, MUL, ADD)
                    for i in range(2):
                        dve.tensor_scalar(qt(1 + i, 0), q_tmp(i), 0.5 / (2 * PI), None, MUL)
                        ins = dve.tensor_scalar(qt(1 + i, 1), q_tmp(i), 0.5 / (2 * PI), 0.25, MUL, ADD)
                elif k == "q_up":
                    ins = dve.tensor_scalar(turns_whole, turns, ROUND, None, ADD)
                elif k == "q_down":
                    ins = dve.tensor_scalar(turns_whole, turns_whole, ROUND, None, SUB)
                elif k == "q_frac":
                    ins = dve.tensor_tensor(turns, turns, turns_whole, SUB)
                elif k == "gate":
                    e, c = divmod(name[1], 2)
                    trig, ang = (qs(0, 1), 1) if e in (0, 3) else (qs(0, 0), 2)
                    other = qs(ang, 1 - c)
                    sign = {(0, 1): -1.0, (1, 0): -1.0, (1, 1): -1.0, (2, 1): -1.0}.get((e, c), 1.0)
                    dst = gate_m[:, c * 32:c * 32 + 32].rearrange("p (g e) -> p g e", e=4)[:, :, e]
                    ins = dve.scalar_tensor_tensor(out=dst, in0=trig, scalar=sign, in1=other, op0=MUL, op1=MUL)
                elif k == "gate_negs":
                    ins = dve.tensor_scalar(gate_m[:, 64:96], gate_m[:, 32:64], -1.0, None, MUL)
                elif k == "kron":
                    ins = kron(name[1], name[2])
                elif k == "m1_copy":
                    ins = dve.tensor_copy(m1, work[0:AMPS, 0:4 * AMPS])
                elif k == "q_neg":
                    ins = dve.tensor_scalar(q_neg, m1[:, 3 * AMPS:4 * AMPS], -1.0, None, MUL)
                elif k == "tt_copy":
                    ins = dve.tensor_copy(ttc, work[0:AMPS, 0:2 * AMPS])
                elif k == "blocks_mask":
                    c = name[1]
                    ins = dve.tensor_tensor(
                        unitary[:, c, :].rearrange("p (j k) -> p j k", k=AMPS),
                        kc("rowmask").unsqueeze(2).broadcast_to([P, CH, AMPS]),
                        work[:, c * AMPS:(c + 1) * AMPS].unsqueeze(1).broadcast_to([P, CH, AMPS]), MUL)
                elif k == "postw_mask":
                    j = name[1]
                    ins = dve.tensor_scalar(postw[:, j, :], work[:, 0:P], kc("rowmask", j, j + 1), None, MUL)
                elif k == "stats":
                    src = NORM[name[1]][0]
                    if name[1] == "0":
                        dve.wait_ge(x_loaded, 16 * s + 16)
                    h = name[2]
                    ins = dve.bn_stats(gn[:, 6 * h:6 * h + 6], src[:, 512 * h:512 * h + 512])
                elif k == "square":
                    ins = dve.tensor_tensor(gn[:, 21:25], stat[:, :, 1], stat[:, :, 1], MUL)
                elif k == "mean_square":
                    ins = dve.scalar_tensor_tensor(out=stat[:, :, 2], in0=stat[:, :, 2], scalar=4.0 / TOK,
                                                   in1=gn[:, 21:25], op0=MUL, op1=ADD)
                elif k == "group_copy":
                    ins = dve.tensor_reduce(gn[:, 14:16],
                                            work[:, 0:12].rearrange("p (i c) -> p c i", c=3)[:, 1:3, :],
                                            AX.X, ADD)
                elif k == "group_negvar":
                    ins = dve.scalar_tensor_tensor(out=gn[:, 17:18], in0=gn[:, 14:15], scalar=gn[:, 14:15],
                                                   in1=gn[:, 15:16], op0=MUL, op1=SUB)
                elif k == "group_eps":
                    ins = dve.tensor_scalar(gn[:, 18:19], gn[:, 17:18], -1.0, 1e-5, MUL, ADD)
                elif k == "group_shift":
                    ins = dve.scalar_tensor_tensor(out=gn[:, 20:21], in0=gn[:, 14:15], scalar=-1.0,
                                                   in1=gn[:, 19:20], op0=MUL, op1=MUL)
                elif k == "norm":
                    _, src, dst = NORM[name[1]]
                    if name[1] == "1" and not (isinstance(s, int) and s == 0):
                        dve.wait_ge(old_kept, 32 * s)
                    ins = dve.tensor_scalar(dst, src, gn[:, 19:20], gn[:, 20:21], MUL, ADD)
                elif k == "add0":
                    ins = dve.scalar_tensor_tensor(out=x_new[:, :], in0=work[:, :], scalar=kc("conv0_b"),
                                                   in1=x_new[:, :], op0=ADD, op1=ADD)
                elif k == "dt_sum":
                    h = name[2]
                    ins = dve.tensor_tensor(dt[:, h, :], dt[:, h, :], du[:, h, :], ADD)
                elif k == "dt_u":
                    _, d, h = name
                    ins = dve.tensor_tensor(du[:, h, :], dt[:, h, :], u_conv[:, d % 2, h, :], MUL)
                elif k == "add1":
                    ins = dve.tensor_tensor(x_old[:, :], x_old[:, :], t0, ADD)
                elif k == "rows":
                    ins = dve.tensor_reduce(um[:, 0:32], tile2d(t0), AX.X, ADD)
                elif k == "cols":
                    ins = dve.tensor_reduce(um[:, 32:64], t0.rearrange("p (a b) -> p b a", b=SIDE), AX.X, ADD)
                elif k == "means":
                    ins = dve.tensor_scalar(um, um, 1.0 / SIDE, None, MUL)
                elif k in ("gate_h", "gate_w"):
                    i = k == "gate_w"
                    ins = dve.tensor_scalar(gate_a[:, 32 * i:32 * i + 32], work[:, 32 * i:32 * i + 32],
                                            kc("gate_b", int(i), i + 1), None, ADD)
                elif k == "gate_sig":
                    ins = dve.tensor_scalar(gate_s, gate_s, 0.5, 0.5, MUL, ADD)
                elif k == "pad2":
                    ins = dve.tensor_copy(upad[:, :, PAD:PAD + SIDE], mh(work[:, 0:128]))
                elif k == "z2":
                    ins = dve.tensor_copy(z2, work[:, 128:256])
                elif k == "taps2":
                    w4 = kc("taps2").rearrange("p (m k) -> p m k", k=TAPS)
                    for i in range(MH):
                        base = upad[:, i, 0:SIDE]
                        ins = dve.tensor_tensor(
                            t1[:, 128 * i:128 * i + 128].rearrange("p (k t) -> p k t", k=TAPS),
                            windows(i), w4[:, i, :].unsqueeze(2).broadcast_to([P, TAPS, SIDE]), MUL)
                elif k == "tapsum2":
                    ins = dve.tensor_reduce(mh(u2), t1[:, 0:512].rearrange("p (m k t) -> p m t k", m=MH, k=TAPS),
                                            AX.X, ADD)
                elif k == "tapbias2":
                    ins = dve.tensor_tensor(mh(u2), mh(u2), per_mh(kc("conv2_b")), ADD)
                elif k == "xcopy2":
                    ins = dve.tensor_copy(dbl[:, :], work[0:XP2, 0:64])
                elif k == "dtbias2":
                    ins = dve.tensor_tensor(mh(dt2), mh(work[:, 0:128]), per_mh(kc("dt2_b")), ADD)
                elif k == "dtsum2":
                    ins = dve.tensor_tensor(dt2, dt2, sp2, ADD)
                elif k == "du2":
                    ins = dve.tensor_tensor(du2, dt2, u2, MUL)
                elif k in ("dta2", "start2", "input2", "scan2", "prod2", "ysum2"):
                    _, m, h = name
                    i = 2 * m + h
                    a, b = t1[:, 0:512], t1[:, 512:1024]
                    nt = lambda ap: ap.rearrange("p (n t) -> p n t", t=SIDE)
                    over_n = lambda ap: mh(ap)[:, i, :].unsqueeze(1).broadcast_to([P, NST, SIDE])
                    if k == "dta2":
                        ins = dve.tensor_tensor(
                            nt(a), over_n(dt2),
                            a_neg2[:, i * NST:(i + 1) * NST].unsqueeze(2).broadcast_to([P, NST, SIDE]), MUL)
                    elif k == "start2":
                        ins = dve.memset(nt(a)[:, :, 0], 0.0)
                    elif k == "input2":
                        ins = dve.tensor_tensor(nt(b), over_n(du2), nt(work[:, 0:512]), MUL)
                    elif k == "scan2":
                        ins = dve.tensor_tensor_scan(a, a, b, 0.0, MUL, ADD)
                    elif k == "prod2":
                        ins = dve.tensor_tensor(b, a, work[:, 512:1024], MUL)
                    else:
                        ins = dve.tensor_reduce(mh(yy2)[:, i, :], b.rearrange("p (n t) -> p t n", t=SIDE), AX.X, ADD)
                elif k == "dterm2":
                    ins = dve.tensor_tensor(mh(sp2), mh(u2), per_mh(kc("D2")), MUL)
                elif k == "dadd2":
                    ins = dve.tensor_tensor(yy2, yy2, sp2, ADD)
                elif k == "yz2":
                    ins = dve.tensor_tensor(yy2, yy2, z2, MUL)
                elif k == "xa":
                    ins = dve.tensor_tensor(xa, work[:, 0:64], gate_a, ADD)
                elif k == "xa_sig":
                    ins = dve.tensor_scalar(xa, xa, 0.5, 0.5, MUL, ADD)
                elif k == "mlp_b":
                    m = name[1]
                    ins = dve.tensor_scalar(xxy[:, 32 * m:32 * m + 32], work[:, 32 * m:32 * m + 32],
                                            kc("mlp2_b", m, m + 1), None, ADD)
                elif k == "outer_h":
                    ins = dve.tensor_tensor(tile2d(t1), gate_s[:, 0:32].unsqueeze(2).broadcast_to([P, SIDE, SIDE]),
                                            xxy[:, 32:64].unsqueeze(1).broadcast_to([P, SIDE, SIDE]), MUL)
                elif k == "outer_w":
                    ins = dve.tensor_tensor(inner, gate_s[:, 32:64].unsqueeze(1).broadcast_to([P, SIDE, SIDE]),
                                            xxy[:, 0:32].unsqueeze(2).broadcast_to([P, SIDE, SIDE]), MUL)
                elif k == "times_x":
                    ins = dve.tensor_tensor(t0, t0, work[:, :], MUL)
                elif k == "add2":
                    ins = dve.tensor_tensor(x_old[:, :], x_old[:, :], t0, ADD)
                elif k == "angle_b":
                    ins = dve.tensor_tensor(circq[:, 0, :, :],
                                            work[:, 0:CH * NQ].rearrange("p (j w) -> p j w", w=NQ),
                                            preb[:, :].unsqueeze(1).broadcast_to([P, CH, NQ]), ADD)
                elif k == "turns":
                    i = name[1]
                    ins = dve.tensor_scalar(circ[:, i, :, :], circq[:, 0, :, :], 0.25, 0.25 * (1 - i), MUL, ADD)
                elif k == "round_up":
                    ins = dve.tensor_scalar(circq[:, :, :, :], circ[:, :, :, :], ROUND, None, ADD)
                elif k == "round_down":
                    ins = dve.tensor_scalar(circq[:, :, :, :], circq[:, :, :, :], ROUND, None, SUB)
                elif k == "fraction":
                    ins = dve.tensor_tensor(circq[:, :, :, :], circ[:, :, :, :], circq[:, :, :, :], SUB)
                elif k == "pair":
                    i = name[1]
                    a = circ[:, :, :, 2 * i].rearrange("p b j -> p j b").unsqueeze(3).broadcast_to([P, CH, 2, 2])
                    b = circ[:, :, :, 2 * i + 1].rearrange("p b j -> p j b").unsqueeze(2).broadcast_to([P, CH, 2, 2])
                    ins = dve.tensor_tensor(sp2[:, 32 * i:32 * i + 32].rearrange("p (j a b) -> p j a b", a=2, b=2),
                                            a, b, MUL)
                elif k == "amplitudes":
                    a = sp2[:, 0:32].rearrange("p (j a) -> p j a", a=4).unsqueeze(3).broadcast_to([P, CH, 4, 4])
                    b = sp2[:, 32:64].rearrange("p (j a) -> p j a", a=4).unsqueeze(2).broadcast_to([P, CH, 4, 4])
                    ins = dve.tensor_tensor(yy2.rearrange("p (j a b) -> p j a b", a=4, b=4), a, b, MUL)
                elif k == "turn_copy":
                    ins = dve.tensor_copy(du2, work[:, 0:P])
                elif k == "result":
                    ins = dve.scalar_tensor_tensor(out=t0, in0=work[:, :], scalar=kc("post_b"),
                                                   in1=x_old[:, :], op0=ADD, op1=ADD)
                ins.then_inc(side, 1)

            def windows(i):
                ap = upad[:, i, 0:SIDE].unsqueeze(1).broadcast_to([P, TAPS, SIDE])
                return bass.AP(ap.tensor, ap.offset, [ap.ap[0], [1, TAPS], [1, SIDE]])

            def angle(i):
                return q_sb[:, 0:3 * GATES].rearrange("p (g a) -> p g a", a=3)[:, :, i]

            def q_tmp(i):
                return q_sb[:, 24 + 8 * i:32 + 8 * i]

            def qt(i, c):
                return q_sb[:, 48 + 16 * i + 8 * c:56 + 16 * i + 8 * c]

            def qs(i, c):
                return sines[:, 16 * i + 8 * c:16 * i + 8 * c + 8]

            def kron(n, part):
                ins = None
                for layer in range(2):
                    if n < 2:
                        size = 2
                        g = 4 * layer + 2 * n
                        a = lambda c: gate_m[:, c * 32 + 4 * g:c * 32 + 4 * g + 4]
                        b = lambda c: gate_m[:, c * 32 + 4 * g + 4:c * 32 + 4 * g + 8]
                        o = (kr01, kr23)[n]
                        dst = lambda c: o[:, c * 32 + 16 * layer:c * 32 + 16 * layer + 16]
                        tmp = krt[:, 64 + 32 * layer:64 + 32 * layer + 32]
                    else:
                        size = 4
                        a = lambda c: kr01[:, c * 32 + 16 * layer:c * 32 + 16 * layer + 16]
                        b = lambda c: kr23[:, c * 32 + 16 * layer:c * 32 + 16 * layer + 16]
                        dst = lambda c: kr[:, c * 512 + 256 * layer:c * 512 + 256 * layer + 256]
                        tmp = scratch[0:1, 5632 + 512 * layer:5632 + 512 * layer + 512]
                    half = size ** 4

                    def times(out_ap, x, y):
                        o4 = out_ap.rearrange("p (i k j l) -> p i k j l", i=size, k=size, j=size)
                        x2 = x.rearrange("p (i j) -> p i j", j=size)
                        y2 = y.rearrange("p (k l) -> p k l", l=size)
                        last = None
                        for i in range(size):
                            last = dve.tensor_tensor(
                                o4[:, i], x2[:, i, :].unsqueeze(1).unsqueeze(3).broadcast_to([1, size, size, size]),
                                y2.unsqueeze(2).broadcast_to([1, size, size, size]), MUL)
                        return last

                    if part == 0:
                        times(dst(0), a(0), b(0))
                        ins = times(dst(1), a(0), b(1))
                    elif part == 1:
                        times(tmp[:, 0:half], a(1), b(1))
                        ins = times(tmp[:, half:2 * half], a(1), b(0))
                    else:
                        dve.tensor_tensor(dst(0), dst(0), tmp[:, 0:half], SUB)
                        ins = dve.tensor_tensor(dst(1), dst(1), tmp[:, half:2 * half], ADD)
                return ins

            dve.wait_ge(weights_in, 16 * 7)

            def walk(steps, at, s):
                for i, (name, e) in enumerate(steps):
                    if e == "D":
                        step(name, at + i, s)

            walk(lead + lead2 + begin, 0, 0)

            def image(kind, s):
                plan, base = plans[kind], start_of(kind, s)
                names = [x[1] for x in plan]

                def take_y(p):
                    f, t, h = p // 4, p // 2 % 2, p % 2
                    if t:
                        dve.wait_ge(sum_done, s * UNITS + (p + 1) * NST)
                        dve.tensor_tensor(yz[:, f, h, :], y_acc[:, :], silu_z[:, h, :], MUL).then_inc(y_taken, 1)

                for u in range(UNITS + 1):
                    if u < UNITS:
                        d, h, n = unit_of(u)
                        if n == 0:
                            dve.wait_ge(side, base + (names.index(("dt_u", d, h)) + 1 if u else 0))
                        dve.wait_ge(b_ready, s * UNITS + u + 1)
                        b = bring[:, u % BRING, :]
                        dve.tensor_tensor(b, du[:, h, :], b, MUL).then_inc(input_ready, 1)
                        dve.wait_ge(input_ready, s * UNITS + u + 1)
                        dve.wait_ge(decay_ready, s * UNITS + u + 1)
                        slot = ring[:, u % RING, :]
                        if d % 2:
                            slot, b = slot[:, ::-1], b[:, ::-1]
                        dve.tensor_tensor_scan(slot, slot, b, 0.0, MUL, ADD).then_inc(scan_done, 1)
                        if u % NST == 2 and u > 2:
                            take_y(u // NST - 1)
                    else:
                        take_y(PASSES - 1)
                    for i, (at, name, e) in enumerate(plan):
                        if at == u and e == "D":
                            step(name, base + i, s + 1 if name in [x[0] for x in front()] else s)
            each_image(dve, image)
            walk(finish, start_of("last", images - 1) + len(plans["last"]), images - 1)

        @block.tensor
        def _(pe):
            def mm(out_ap, w, x, start, stop):
                return pe.matmul(out_ap, w, x, start=start, stop=stop, skip_group_check=True)

            def halves(w, x, start=True, stop=True, rows=P, out_t=None):
                for c in range(2):
                    ins = mm((work if out_t is None else out_t)[0:rows, c * BANK:(c + 1) * BANK], w, x(c),
                             start, stop)
                return ins

            def flat(ap):
                return lambda c: ap[:, c * BANK:(c + 1) * BANK]

            def step(name, pos, s):
                pe.wait_ge(side, pos)
                k = name[0]
                if k == "mixw":
                    _, f, h = name
                    ins = mm(work[:, 0:P], oc("outp", f * DI + h * P, f * DI + (h + 1) * P), kc("nin2"), True, True)
                elif k == "m1":
                    pe.wait_ge(matrices_in, 16 * 4)
                    for c in range(2):
                        mm(work[0:AMPS, c * AMPS:(c + 1) * AMPS], oc("perm1", rows=AMPS),
                           lay[:, c * AMPS:(c + 1) * AMPS], True, True)
                        ins = mm(work[0:AMPS, (2 + c) * AMPS:(3 + c) * AMPS],
                                 lay[:, (2 + c) * AMPS:(3 + c) * AMPS], oc("perm2", rows=AMPS), True, True)
                elif k == "tt":
                    m = [m1[:, i * AMPS:(i + 1) * AMPS] for i in range(4)]
                    mm(work[0:AMPS, 0:AMPS], m[0], m[2], True, False)
                    mm(work[0:AMPS, 0:AMPS], m[1], q_neg, False, True)
                    mm(work[0:AMPS, AMPS:2 * AMPS], m[0], m[3], True, False)
                    ins = mm(work[0:AMPS, AMPS:2 * AMPS], m[1], m[2], False, True)
                elif k == "blocks":
                    ins = mm(work[:, 0:2 * AMPS], oc("rep", rows=AMPS), ttc, True, True)
                elif k == "postw":
                    ins = mm(work[:, 0:P], oc("sign", rows=NQ), oc("post", rows=NQ), True, True)
                elif k == "group_mean":
                    ins = mm(work[:, 0:12], kc("gavg"), gn[:, 0:12], True, True)
                elif k == "conv0":
                    i, j = divmod(name[1], 3)
                    ins = halves(kc("conv0", name[1] * P, (name[1] + 1) * P),
                                 lambda c: padded[:, i + 16 * c:i + 16 * c + 16, j:j + SIDE],
                                 name[1] == 0, name[1] == 8)
                elif k == "nin":
                    ins = halves(kc("nin"), flat(h_mid))
                elif k == "conv_in":
                    _, d, h, j = name
                    off = 2 * PAD - j if d % 2 else j
                    ins = halves(fused[:, d // 2, j, h * P:(h + 1) * P], flat(h_new[:, off:off + TOK]),
                                 j == 0, j == TAPS - 1)
                elif k == "z":
                    _, d, h = name
                    lo = d // 2 * DI + h * P
                    ins = halves(kc("z", lo, lo + P), flat(h_mid))
                elif k == "xproj":
                    _, d, c = name
                    for h in range(HALVES):
                        ins = mm(work[0:XP, c * BANK:(c + 1) * BANK], kc("xproj", h * XP, (h + 1) * XP),
                                 u_conv[:, d % 2, h, c * BANK:(c + 1) * BANK], h == 0, h == HALVES - 1)
                elif k == "rest":
                    _, d, i = name
                    r = slice(32 * i, 32 * i + 32)
                    ins = halves(negsel[r, :], flat(stack[r, d % 2, :]), False, True, rows=96)
                elif k == "dt_proj":
                    h = name[2]
                    ins = halves(dtw_sb[DTP:DTP + RANK, h * P:(h + 1) * P], flat(dt_rows))
                elif k == "c_spread":
                    _, d, n = name
                    ins = halves(sel[0:96, NST + n:NST + n + 1].broadcast_to([96, P]),
                                 flat(stack[0:96, d % 2, :]))
                elif k == "mix":
                    i = name[1]
                    if i < 4:
                        if i == 0:
                            pe.wait_ge(y_taken, PASSES * s)
                        ins = halves(mixw[:, i // 2, i % 2, :], flat(yz[:, i // 2, i % 2, :]), i == 0, False)
                    else:
                        pe.wait_ge(old_kept, 32 * s)
                        ins = halves(kc("nin2"), flat(h_old[:, :]), False, True)
                elif k == "squeeze":
                    ins = mm(work[0:RANK, 0:64], kc("squeeze"), um, True, True)
                elif k == "gates":
                    mm(work[:, 0:32], s8("spread_h"), g8[:, 0:32], True, True)
                    ins = mm(work[:, 32:64], s8("spread_w"), g8[:, 32:64], True, True)
                elif k == "in2":
                    for m in range(2):
                        for i in range(4):
                            h = i % 2
                            col = (i // 2) * 128 + (2 * m + h) * 32
                            ins = mm(work[:, col:col + 32], kc("in2", m * 2 * DI + i * P, m * 2 * DI + (i + 1) * P),
                                     um[:, 32 * m:32 * m + 32], True, True)
                elif k == "xproj2":
                    for m in range(2):
                        for h in range(HALVES):
                            i = 2 * m + h
                            ins = mm(work[0:XP2, 32 * m:32 * m + 32], kc("xproj2", i * XP2, (i + 1) * XP2),
                                     mh(u2)[:, i, :], h == 0, h == 1)
                elif k == "dtproj2":
                    for i in range(MH):
                        ins = mm(work[:, 32 * i:32 * i + 32], s8("dtp2", i * P, (i + 1) * P),
                                 dbl[0:RANK, 32 * (i // 2):32 * (i // 2) + 32], True, True)
                elif k == "spread2":
                    _, m, q = name
                    for n in range(8 * q, 8 * q + 8):
                        row = RANK + n
                        ins = mm(work[:, 32 * n:32 * n + 32],
                                 kc("ident", row, row + 1)[0:XP2, :].broadcast_to([XP2, P]),
                                 dbl[:, 32 * m:32 * m + 32], True, True)
                elif k == "out2":
                    for m in range(2):
                        for h in range(HALVES):
                            i = 2 * m + h
                            ins = mm(work[:, 32 * m:32 * m + 32], kc("out2", i * P, (i + 1) * P), mh(yy2)[:, i, :],
                                     h == 0, h == 1)
                elif k in ("mlp1", "mlp2"):
                    src = xa if k == "mlp1" else ml
                    for m, a in enumerate("xy"):
                        ins = mm(work[:, 32 * m:32 * m + 32], kc(k + a), src[:, 32 * m:32 * m + 32], True, True)
                elif k == "adjust":
                    i = name[1]
                    ins = halves(kc("adjust", i * P, (i + 1) * P),
                                 (lambda c: inner[:, 16 * c:16 * c + 16, :]) if i else flat(t1), i == 0, i == 1)
                elif k == "angles":
                    for j in range(CH):
                        ins = mm(work[:, NQ * j:NQ * j + NQ], t0[:, j * P:(j + 1) * P], kc("pre"), True, True)
                elif k == "turn":
                    ins = mm(work[:, 0:P], yy2, kc("ident"), True, True)
                elif k == "unitary":
                    for c in range(2):
                        ins = mm(work[:, c * P:(c + 1) * P], unitary[:, c, :], du2, True, True)
                elif k == "post":
                    for j in range(4 * name[1], 4 * name[1] + 4):
                        for c in range(2):
                            ins = mm(work[:, j * P:(j + 1) * P], postw[:, j, :], t0[:, c * P:(c + 1) * P], c == 0, c == 1)
                ins.then_inc(side, 1)

            def walk(steps, at, s):
                for i, (name, e) in enumerate(steps):
                    if e == "P":
                        step(name, at + i, s)

            walk(lead + lead2 + begin, 0, 0)

            def image(kind, s):
                plan, base = plans[kind], start_of(kind, s)
                names = [x[1] for x in plan]

                def spread_b(u):
                    d, h, n = unit_of(u)
                    if h == 0 and n == 0:
                        pe.wait_ge(side, base + (names.index(("part", d, 2)) + 1 if u else 0))
                    if u >= BRING or not (isinstance(s, int) and s == 0):
                        pe.wait_ge(scan_done, s * UNITS + u - BRING + 1)
                    halves(sel[0:96, n:n + 1].broadcast_to([96, P]), flat(stack[0:96, d % 2, :]),
                           out_t=bring[:, u % BRING, :]).then_inc(b_ready, 1)

                def add_y(u):
                    d, h, n = unit_of(u)
                    if n == 0:
                        if u or not (isinstance(s, int) and s == 0):
                            pe.wait_ge(y_taken, s * PASSES + u // NST)
                        halves(diag_d[:, h, :], flat(u_conv[:, d % 2, h, :]), True, False, out_t=y_acc)
                        if d % 2:
                            halves(kc("ident"), flat(yz[:, d // 2, h, :]), False, False, out_t=y_acc)
                    pe.wait_ge(prod_ready, s * UNITS + u + 1)
                    halves(kc("ident"), flat(ring[:, u % RING, :]), False, n == NST - 1,
                           out_t=y_acc).then_inc(sum_done, 1)

                spread_b(0)
                for u in range(UNITS + 1):
                    if u + 1 < UNITS:
                        spread_b(u + 1)
                    if 2 <= u < UNITS:
                        add_y(u - 2)
                    if u == UNITS:
                        add_y(UNITS - 2)
                        add_y(UNITS - 1)
                    for i, (at, name, e) in enumerate(plan):
                        if at == u and e == "P":
                            step(name, base + i, s)
            each_image(pe, image)
            walk(finish, start_of("last", images - 1) + len(plans["last"]), images)


def layout(inp):
    a = {k: np.asarray(v) for k, v in inp.items()}
    L1 = {k[8:]: v for k, v in a.items() if k.startswith("L1_conv_")}
    L2 = {k[8:]: v for k, v in a.items() if k.startswith("L2_conv_")}
    L3 = {k[8:]: v for k, v in a.items() if k.startswith("L3_conv_")}
    col = lambda v: v.reshape(-1, P).T
    eye = np.eye(P, dtype=np.float32)
    w_in = L1["in_proj_w"].T
    xp = L1["x_proj_w"].T
    xproj = []
    for h in range(HALVES):
        r = xp[h * P:(h + 1) * P]
        xproj += [r[:, RANK:]] * 3 + [r[:, :RANK]]
    halfcols = lambda m: [m[h * P:(h + 1) * P] for h in range(HALVES)]
    neg = np.zeros((P, 96), np.float32)
    for i in range(96):
        for j in range(3):
            neg[i, i % 32 + 32 * j] = -1.0
    keep = {
        "conv0": [a["L0_conv_weight"].transpose(1, 2, 3, 0).reshape(P, 9 * P)],
        "nin": [L1["nin_w"].T], "z": [w_in[:, DI:], w_in[::-1, DI:]], "xproj": xproj,
        "nin2": [L1["nin2_w"].T], "ident": [eye],
        "gavg": [np.kron(np.eye(P // GROUP, dtype=np.float32), np.full((GROUP, GROUP), 1 / (4 * GROUP), np.float32))],
        "alog": halfcols(L1["A_log"]), "conv0_b": [col(a["L0_conv_bias"])], "conv_b": [col(L1["conv_b"])],
        "dt_b": [col(L1["dt_proj_b"])], "D": [col(L1["D"])],
        "bn1": [col(L1["bn1_" + k]) for k in "gbmv"], "bn2": [col(L1["bn2_" + k]) for k in "gbmv"],
        "squeeze": [L2["conv1_w"].T], "mlp1x": [L2["mlpx_w1"].T], "mlp1y": [L2["mlpy_w1"].T],
        "mlp2x": [L2["mlpx_w2"].T], "mlp2y": [L2["mlpy_w2"].T],
        "adjust": [L2["adjust_w"][:, :P].T, L2["adjust_w"][:, P:].T],
        "in2": [L2["mx_in_w"].T, L2["my_in_w"].T],
        "taps2": [m for w in ("mx", "my") for m in halfcols(L2[w + "_conv_w"][:, 0])],
        "conv2_b": [col(L2["mx_conv_b"]), col(L2["my_conv_b"])],
        "xproj2": [m for w in ("mx", "my") for m in halfcols(L2[w + "_xproj_w"].T)],
        "dt2_b": [col(L2["mx_dt_b"]), col(L2["my_dt_b"])],
        "alog2": [m for w in ("mx", "my") for m in halfcols(L2[w + "_Alog"])],
        "D2": [col(L2["mx_D"]), col(L2["my_D"])],
        "out2": [m for w in ("mx", "my") for m in halfcols(L2[w + "_out_w"].T)],
        "gate_b": [col(L2["convh_b"]), col(L2["convw_b"])],
        "mlp1_b": [col(L2["mlpx_b1"]), col(L2["mlpy_b1"])], "mlp2_b": [col(L2["mlpx_b2"]), col(L2["mlpy_b2"])],
        "pre": [L3["pre_w"].T], "post_b": [col(L3["post_b"])], "negstack": [neg],
        "rowmask": [np.kron(np.eye(CH, dtype=np.float32), np.ones((AMPS, 1), np.float32))],
    }

    def tall(m):
        out = np.zeros((P, m.shape[1]), np.float32)
        out[:m.shape[0]] = m
        return out

    def perm_t(layer):
        m = np.zeros((AMPS, AMPS), np.float32)
        for k, to in enumerate(circuit_entangler(layer)):
            m[k, to] = 1.0
        return m

    sign = np.array([[1.0 - 2.0 * (i % AMPS >> NQ - 1 - w & 1) for i in range(P)] for w in range(NQ)], np.float32)
    once = {
        "in": [w_in[:, :DI], w_in[::-1, :DI]], "outp": [L1["out_proj_w"], L1["out_proj_w"][::-1]],
        "perm1": [tall(perm_t(0))], "perm2": [tall(perm_t(1))],
        "rep": [tall(np.tile(np.eye(AMPS, dtype=np.float32), (1, CH)))], "sign": [tall(sign)],
        "post": [tall(L3["post_w"].T)],
    }
    small = {
        "spread_h": [L2["convh_w"].T], "spread_w": [L2["convw_w"].T],
        "dtp2": [L2["mx_dt_w"].T, L2["my_dt_w"].T], "bn": [L2["bn_" + k][:, None] for k in "gbmv"],
        "squeeze_b": [L2["conv1_b"][:, None]],
    }
    pack = lambda table, parts: np.ascontiguousarray(
        np.concatenate([m for name, _ in table for m in parts[name]], axis=1))
    return {
        "x": a["x"].reshape(a["x"].shape[0], P, TOK), "keep": pack(KEEP, keep), "once": pack(ONCE, once),
        "small": pack(SMALL, small), "dtw": np.ascontiguousarray(L1["dt_proj_w"].T),
        "conv_wt": np.ascontiguousarray(L1["conv_w"].T).reshape(TAPS * DI),
        "preb": L3["pre_b"], "qw": L3["q_weights"].reshape(1, -1),
    }


def kernel(**inputs):
    import concourse.bacc as bacc
    from concourse.bass_utils import run_bass_kernel_spmd

    laid = layout(inputs)
    images = laid["x"].shape[0]
    nc = bacc.Bacc("TRN2", target_bir_lowering=False, num_devices=1)
    arrays = {f"in_{k}": v for k, v in laid.items()}
    aps = {k: nc.dram_tensor(f"in_{k}", list(v.shape), F32, kind="ExternalInput").ap() for k, v in laid.items()}
    out = nc.dram_tensor("out_0", [images, P, TOK], F32, kind="ExternalOutput").ap()
    four_layers(nc, images, aps["x"], aps["keep"], aps["once"], aps["small"], aps["dtw"], aps["conv_wt"],
                aps["preb"], aps["qw"], out)
    r = run_bass_kernel_spmd(nc, [arrays], core_ids=[0])
    return np.asarray(r.results[0]["out_0"]).reshape(images, P, SIDE, SIDE)
```

```python
from contextlib import ExitStack

import numpy as np
import concourse.bass as bass
from concourse import mybir

F32 = mybir.dt.float32
BF16 = mybir.dt.bfloat16
ALU = mybir.AluOpType
ACT = mybir.ActivationFunctionType
AX = mybir.AxisListType

P, SIDE = 128, 32
TOK = SIDE * SIDE
BANK = 512
HALVES = 2
DI = HALVES * P
NST = 16
RANK = 8
TAPS = 4
PAD = TAPS - 1
DIRS = 4
PASSES = DIRS * HALVES
UNITS = PASSES * NST
RING = 4
BRING = 2
PARTS = 3
DTP = 32 * PARTS
CP = DTP + RANK
XP = CP + NST
CGROUP = 4
XP2 = RANK + 2 * NST
MH = 4
NQ = 4
GATES = 2 * NQ
AMPS = 2 ** NQ
CH = TOK // P
GROUP = 4
PI = float(np.pi)
TWO_PI = 6.283185
ROUND = 1.5 * 2 ** 23

KEEP = [
    ("conv0", 9 * P), ("nin", P), ("z", 2 * DI), ("xproj", HALVES * XP), ("nin2", P), ("ident", P),
    ("gavg", P), ("alog", HALVES * NST), ("conv0_b", 1), ("conv_b", HALVES), ("dt_b", HALVES),
    ("D", HALVES), ("bn1", 4), ("bn2", 4), ("squeeze", 8), ("mlp1x", P), ("mlp1y", P), ("mlp2x", P),
    ("mlp2y", P), ("adjust", 2 * P), ("in2", 2 * 2 * DI), ("taps2", MH * TAPS), ("conv2_b", MH),
    ("xproj2", MH * XP2), ("dt2_b", MH), ("alog2", MH * NST), ("D2", MH), ("out2", MH * P),
    ("gate_b", 2), ("mlp1_b", 2), ("mlp2_b", 2), ("pre", NQ), ("post_b", 1), ("negstack", 96),
    ("rowmask", CH),
]
ONCE = [("in", 2 * DI), ("outp", 2 * DI), ("perm1", AMPS), ("perm2", AMPS), ("rep", P), ("sign", P),
        ("post", P)]
SMALL = [("spread_h", P), ("spread_w", P), ("dtp2", 2 * DI), ("bn", 4), ("squeeze_b", 1)]


def columns(table):
    at, out = 0, {}
    for name, width in table:
        out[name] = (at, at + width)
        at += width
    return out, at


def circuit_entangler(layer):
    r = layer % (NQ - 1) + 1
    to = list(range(AMPS))
    for w in range(NQ):
        c, t = NQ - 1 - w, NQ - 1 - (w + r) % NQ
        to = [k ^ (1 << t) if k >> c & 1 else k for k in to]
    return to


OTHER_TABLES = ("q_sin", "squeeze_gelu", "gate_tanh", "silu2", "xa_tanh", "mlp_gelu",
                "sine")


def norm(tag):
    return [(("stats", tag, 0), "D"), (("stats", tag, 1), "D"), (("square", tag), "D"),
            (("mean_square", tag), "D"), (("group_mean", tag), "P"), (("group_copy", tag), "D"),
            (("group_negvar", tag), "D"), (("group_eps", tag), "D"), (("group_rstd", tag), "G"),
            (("group_shift", tag), "D"), (("norm", tag), "D")]


def front():
    s = norm("0")
    for c in range(2):
        s += [(("conv0", k, c), "P") for k in range(9)] + [(("add0", c), "D")]
    s += norm("1")
    for c in range(2):
        s += [(("nin", c), "P"), (("h1", c), "A")]
    return s


def silu(of, d, h, c):
    return [(("silu_exp", d, h, c, of), "A"), (("silu_ln", d, h, c, of), "A"), (("silu_inv", d, h, c, of), "A"),
            (("silu_" + of, d, h, c), "D")]


def operands(d):
    steps = []
    for h in range(HALVES):
        for c in range(2):
            steps += [(("conv_in", d, h, k, c), "P") for k in range(TAPS)] + silu("u", d, h, c)
    if d % 2:
        for h in range(HALVES):
            for c in range(2):
                steps += [(("z", d, h, c), "P")] + silu("z", d, h, c)
    for c in range(2):
        steps += [(("xproj", d, c, h), "P") for h in range(HALVES)]
        steps += [(("part", d, 0, c), "A"), (("dt_c_rows", d, c), "A"), (("rest", d, 0, c), "P"),
                  (("part", d, 1, c), "A"), (("rest", d, 1, c), "P"), (("part", d, 2, c), "A")]
    return steps


def timestep(d, h):
    steps = []
    for c in range(2):
        steps += [(("dt_proj", d, h, c), "P"), (("dt_abs", d, h, c), "A"), (("dt_relu", d, h, c), "A")]
    return steps + [(("dt_exp", d, h), "A"), (("dt_ln", d, h), "A"), (("dt_sum", d, h), "D"), (("dt_u", d, h), "D")]


def turn_y(which, f, h):
    return [x for c in range(2) for x in ((("turn_y", which, f, h, c), "P"), (("turned_y", which, f, h, c), "A"))]


def mix():
    steps = turn_y("before", 1, 1)
    for c in range(2):
        steps += [(("mix", k, c), "P") for k in range(5)] + [(("relu2", c), "A")]
    return steps + [(("add1",), "D")]


def back():
    s = norm("2")
    s += [((k,), "D") for k in ("rows", "cols", "means")]
    s += [(("squeeze",), "P"), (("squeeze_gelu",), "A"), (("gates",), "P"), (("gate_h",), "D"),
          (("gate_w",), "D"), (("gate_tanh",), "A"), (("gate_sig",), "D"), (("in2",), "P"),
          (("pad2",), "D"), (("z2",), "D"), (("taps2",), "D"), (("tapsum2",), "D"),
          (("tapbias2",), "D"), (("silu2",), "A"), (("xproj2",), "P"), (("xcopy2",), "D"),
          (("dtproj2",), "P"), (("dtbias2",), "D"), (("dtabs2",), "A"), (("dtrelu2",), "A"),
          (("dtexp2",), "A"), (("dtln2",), "A"), (("dtsum2",), "D"), (("du2",), "D")]
    for m in range(2):
        for h in range(HALVES):
            s += [(("spread2", m, h, 0), "P"), (("dta2", m, h), "D"), (("input2", m, h), "D"),
                  (("decay2", m, h), "A"), (("spread2", m, h, 1), "P"), (("start2", m, h), "D"),
                  (("scan2", m, h), "D"), (("prod2", m, h), "D"), (("ysum2", m, h), "D")]
    s += [(("dterm2",), "D"), (("dadd2",), "D"), (("yz2",), "D"), (("out2",), "P"), (("xa",), "D"),
          (("xa_tanh",), "A"), (("xa_sig",), "D"), (("mlp1",), "P"), (("mlp_gelu", 0), "A"),
          (("mlp_gelu", 1), "A"), (("mlp2",), "P"), (("mlp_b", 0), "D"), (("mlp_b", 1), "D"),
          (("outer_h",), "D"), (("outer_w",), "D")]
    for c in range(2):
        s += [(("adjust", i, c), "P") for i in range(2)] + [(("times_x", c), "D")]
    s += [(("add2",), "D")] + norm("3")
    s += [(("angles",), "P"), (("angle_b",), "D"), (("turns", 1), "D"), (("turns", 0), "D"),
          (("round_up",), "D"), (("round_down",), "D"), (("fraction",), "D"), (("sine",), "A"),
          (("pair", 0), "D"), (("pair", 1), "D"), (("amplitudes",), "D"), (("turn",), "P"),
          (("turn_copy",), "D"), (("unitary",), "P"), (("probability",), "A")]
    for c in range(2):
        s += [(("post", c), "P"), (("result", c), "D")]
    return s


def setup():
    s = [(("zero",), "G"), (("small_bf16",), "D"), (("conv_neg",), "D")]
    s += [(("fuse", f, k), "D") for f in range(2) for k in range(TAPS)]
    s += [(("diag", h), "D") for h in range(HALVES)]
    s += [(("a_exp",), "A"), (("a_exp2",), "A"), (("a_neg",), "D"), (("a_neg2",), "D")]
    for b in ("bn1", "bn2", "bn"):
        s += [(("bn_eps", b), "D"), (("bn_rstd", b), "G"), (("bn_scale", b), "D"), (("bn_ms", b), "D"),
              (("bn_shift", b), "D")]
    s += [(("bn_bias",), "D"), (("bn_bias2",), "D")]
    for f in range(2):
        for h in range(HALVES):
            s += [(("mixw", f, h), "P"), (("mixw_copy", f, h), "D")]
    s += [((k,), "D") for k in ("q_sum", "q_diff", "q_quarter", "q_up", "q_down", "q_frac")]
    s += [(("q_sin",), "A")]
    s += [(("gate", k), "D") for k in range(8)] + [(("gate_negs",), "D")]
    for n in range(3):
        s += [(("kron", n, 0), "D"), (("kron", n, 1), "D"), (("kron", n, 2), "D")]
    return s


def setup2():
    s = [(("m1",), "P"), (("m1_copy",), "D"), (("q_neg",), "D"), (("tt",), "P"), (("tt_copy",), "D"),
         (("blocks",), "P"), (("blocks_mask", 0), "D"), (("blocks_mask", 1), "D"), (("postw",), "P")]
    s += [(("postw_mask", j), "D") for j in range(CH)]
    return s


LONG = {"conv_in": .85, "xproj": .85, "z": .85, "dt_proj": .85, "mix": .85, "conv0": .85, "nin": .85,
        "adjust": .85, "turn_y": .43, "rest": .2, "dtproj2": .3, "in2": .5, "spread2": 1.2, "unitary": .4,
        "post": .85, "silu_exp": .6, "silu_ln": .6, "silu_inv": .6, "silu_u": .9, "silu_z": .6,
        "dt_c_rows": .6, "part": .6, "dt_abs": .6, "dt_relu": .6,
        "dt_exp": 1., "dt_ln": 1., "turned_y": .6, "h1": .6, "relu2": .6, "squeeze_gelu": 2.7,
        "gate_tanh": 2.7, "silu2": 2.9, "xa_tanh": 2.7, "mlp_gelu": 2.7, "sine": 2.7, "decay2": .6,
        "dt_sum": 1.1, "dt_u": 1.1, "stats": .6, "norm": .6, "add0": .6, "add1": 1.1, "rows": 1.1,
        "cols": 1.1, "taps2": .8, "tapsum2": .6, "dta2": .6, "input2": .6, "scan2": .6, "prod2": .6,
        "ysum2": .6, "outer_h": 1.1, "outer_w": 1.1, "times_x": .6, "add2": 1.1, "result": .6}
BEGINS = {"P": 1.3, "D": 2.6, "A": 3.0, "G": 4.5}
MAIN = {"P": 1.3, "D": 2.3, "A": 1.0, "G": 2.3}
SLACK = {"P": 1.3, "D": 1.2, "A": 2.0, "G": .5}
LANE1_LATER = 0.8
LENGTH = 2.4
MIX_STEPS = ("turn_y", "turned_y", "mix", "relu2")


def lay(lanes, length):
    plan, busy, of = [], {}, {}
    at, done, left = [0, 0], [0.0, 0.0], [list(x) for x in lanes]

    def first_fit(lane):
        earliest, name, e = left[lane][0]
        cost, slot = LONG.get(name[0], .15), max(at[lane], earliest)
        while True:
            begin = slot * length + BEGINS[e]
            start = max(begin, done[lane] + .1)
            if e in busy:
                slot = max(slot, of[e])
                start = max(start, busy[e] + max(0, slot - of[e]) * MAIN[e])
            if start + cost <= begin + length - MAIN[e] + SLACK[e] or start <= begin + .3:
                return start, slot, cost
            slot += 1

    while left[0] or left[1]:
        even = left[1] and left[1][0][1][0] in MIX_STEPS and not (plan and plan[-1][0] > NST)
        later = (0, -.01 if even else LANE1_LATER)
        _, start, slot, cost, lane = min((first_fit(i)[0] + later[i], *first_fit(i), i) for i in range(2) if left[i])
        _, name, e = left[lane].pop(0)
        slot = max(slot, plan[-1][0] if plan else 0)
        plan.append((slot, name, e, lane))
        busy[e], of[e], at[lane], done[lane] = start + cost, slot, slot, start + cost
    return plan


FRONT_FROM = 84


def image_plan(first, last):
    def on(earliest, steps):
        return [(earliest if not i else 0, name, e) for i, (name, e) in enumerate(steps)]

    start = [] if last else front()
    half = 0 if last else [x[0] for x in start].index(("conv0", 0, 1))
    lane0, lane1 = [], []
    for d in range(DIRS):
        slot = 2 * NST * d
        lane0 += on(slot, timestep(d, 1))
        if d == DIRS - 1:
            lane0 += on(0, start[half:])
        if last and d == DIRS - 1:
            continue
        nxt = (d + 1) % DIRS
        lane0 += on(slot, operands(nxt)) + on(slot + NST + 1, timestep(nxt, 0))
        if d == 2:
            lane0 += on(FRONT_FROM, start[:half])
    if not first:
        lane1 += on(0, mix()) + on(0, back())
    lane1 += on(52, turn_y("this", 0, 0)) + on(68, turn_y("this", 0, 1)) + on(116, turn_y("this", 1, 0))
    due = [(("dt_u", d, 1), 2 * NST * d + NST - 3) for d in range(DIRS)]
    if not last:
        due += [(("dt_u", 0, 0), UNITS - 3)]
    due += [(("dt_u", d, 0), 2 * NST * d - 3) for d in range(1, DIRS)]
    due += [(("part", d, 2, 1), 2 * NST * d - 2) for d in range(1, DIRS)]
    if not first:
        due += [(("mix", 4, 1), NST + 1), (("result", 1), UNITS - 3 * NST)]
    length = LENGTH
    while length < 50:
        plan = lay((lane0, lane1), length)
        slot_of = {x[1]: x[0] for x in plan}
        if plan[-1][0] < UNITS and all(slot_of[n] <= by for n, by in due):
            return plan
        length *= 1.02
    raise ValueError("the steps do not fit")


def four_layers(nc, images, x_in, keep, once, small, dtw, conv_wt, preb_row, qw, out):
    KC, keep_w = columns(KEEP)
    OC, once_w = columns(ONCE)
    SC, small_w = columns(SMALL)
    lead = setup()
    lead2 = setup2()
    begin = front() + operands(0) + timestep(0, 0)
    plans = {"first": image_plan(True, images == 1), "mid": image_plan(False, False),
             "last": image_plan(False, True)}
    finish = [(0, name, e, 1) for name, e in mix() + back()]
    before = [(0, name, e, 0) for name, e in lead + lead2 + begin]
    lead2_at, begin_at = len(lead), len(lead) + len(lead2)

    def count(steps, e):
        return sum(x[2] == e for x in steps)

    def bases(kind, s):
        ahead = before if kind == "first" else before + plans["first"]
        if kind == "first":
            return {e: count(ahead, e) for e in "PADG"}
        return {e: count(ahead, e) + (s - 1) * count(plans["mid"], e) for e in "PADG"}

    def nth(steps, i):
        return steps[i][2], count(steps[:i + 1], steps[i][2])

    def nth_named(steps, name):
        return nth(steps, [x[1] for x in steps].index(name))

    def step_before(steps, i):
        for j in range(i - 1, -1, -1):
            if steps[j][3] == steps[i][3]:
                return nth(steps, j)
        return ("D", "A")[steps[i][3]], 0

    with ExitStack() as ctx:
        def sb(name, shape, dt=F32):
            return ctx.enter_context(nc.sbuf_tensor(name, shape, dt))

        def sem(name):
            return ctx.enter_context(nc.semaphore(name))

        c_dram = nc.dram_tensor("c_rows_scratch", [DIRS, NST * TOK], F32).ap()

        c_all = sb("c_all", [P, NST, TOK])
        u_conv = sb("u_conv", [P, 2, HALVES, TOK])
        dt = sb("dt", [P, HALVES, TOK])
        du = sb("du", [P, HALVES, TOK])
        ring = sb("ring", [P, RING, TOK])
        silu_z = sb("silu_z", [P, HALVES, TOK])
        yz = sb("yz", [P, 2, HALVES, TOK])
        x_new = sb("x_new", [P, TOK])
        x_old = sb("x_old", [P, TOK])
        h_new = sb("h_new", [P, TOK + 2 * PAD])
        h_old = sb("h_old", [P, TOK])
        padded = sb("padded", [P, SIDE + 2, SIDE + 2])
        stack = sb("stack", [P, 2, TOK], BF16)
        wk = sb("wk", [P, keep_w])
        smallw = sb("smallw", [P, small_w])
        fused = sb("fused", [P, 2, TAPS, DI])
        diag_d = sb("diag_d", [P, HALVES, P])
        mixw = sb("mixw", [P, 2, HALVES, P])
        unitary = sb("unitary", [P, 2, P])
        postw = sb("postw", [P, CH, P])
        a_neg = sb("a_neg", [P, HALVES * NST])
        a_neg2 = sb("a_neg2", [P, MH * NST])
        sel = sb("sel", [P, 96], BF16)
        negsel = sb("negsel", [P, 96], BF16)
        preb = sb("preb", [P, NQ])
        neghalf = sb("neghalf", [P, 1])
        bnw = sb("bnw", [P, 3, 8])
        conv_neg = sb("conv_neg", [P, HALVES])
        gn_lanes = sb("gn", [P, 2, 32])
        s64 = sb("s64", [P, 8, 64])
        m128 = sb("m128", [P, 6, 128])
        upad = sb("upad", [P, MH, SIDE + PAD])
        g8 = sb("g8", [RANK, 64])
        dbl = sb("dbl", [XP2, 64])
        circ = sb("circ", [P, 2, CH, NQ])
        circq = sb("circq", [P, 2, CH, NQ])

        rows = stack[:, :, :].rearrange("p a t -> p (a t)").bitcast(F32)
        dt_c_rows, dt_rows, c_rows = rows[DTP:XP, :], rows[DTP:CP, :], rows[CP:XP, :]
        dtw_sb = smallw[:, 0:DI]
        bring = ctx.enter_context(nc.psum_tensor("bring", [P, BRING, TOK], F32))
        y_acc = ctx.enter_context(nc.psum_tensor("y_acc", [P, TOK], F32))
        work = ctx.enter_context(nc.psum_tensor("work", [P, TOK], F32))
        w0, w1 = work[:, 0:BANK], work[:, BANK:TOK]

        side = {e: sem("side_" + e) for e in "PADG"}
        weights_in = sem("weights_in")
        b_ready = sem("b_ready")
        decay_ready = sem("decay_ready")
        input_ready = sem("input_ready")
        scan_done = sem("scan_done")
        prod_ready = sem("prod_ready")
        sum_done = sem("sum_done")
        y_taken = sem("y_taken")
        x_loaded = sem("x_loaded")
        old_kept = sem("old_kept")
        out_stored = sem("out_stored")
        matrices_in = sem("matrices_in")
        c_out = sem("c_out")
        c_in = [sem(f"c_in{g}") for g in range(NST // CGROUP)]

        def kc(name, a=0, b=None):
            lo, hi = KC[name]
            return wk[:, lo + a:(hi if b is None else lo + b)]

        def s8(name, a=0, b=None):
            lo, hi = SC[name]
            return smallw[0:RANK, lo + a:(hi if b is None else lo + b)]

        scratch = c_all[:, :, :].rearrange("p n t -> p (n t)")
        once_sb = scratch[:, 0:once_w]
        conv_rows = scratch[:, 2048:2048 + TAPS * DI]
        q_sb = scratch[0:1, 3072:3072 + 16 * GATES]
        turns, turns_whole = q_sb[:, 48:96], scratch[0:1, 3408:3408 + 48]
        sines = scratch[0:1, 4608:4608 + 48]
        gate_m = scratch[0:1, 3200:3200 + 3 * 4 * GATES]
        kr01 = scratch[0:1, 3328:3328 + 3 * 2 * AMPS]
        kr23 = scratch[0:1, 3456:3456 + 3 * 2 * AMPS]
        kr = scratch[0:1, 3584:3584 + 2 * 2 * AMPS * AMPS]
        krt = scratch[0:1, 4608:4608 + 512]
        lay = scratch[0:AMPS, 5120:5120 + 5 * AMPS]
        m1 = scratch[0:AMPS, 5248:5248 + 4 * AMPS]
        q_neg = scratch[0:AMPS, 5312:5312 + AMPS]
        ttc = scratch[0:AMPS, 5376:5376 + 2 * AMPS]

        def oc(name, a=0, b=None, rows=P):
            lo, hi = OC[name]
            return once_sb[0:rows, lo + a:(hi if b is None else lo + b)]

        t0 = yz[:, 1, 0, :]
        t1 = yz[:, 1, 1, :]
        inner = padded[:, 1:SIDE + 1, 1:SIDE + 1]
        h_mid = h_new[:, PAD:PAD + TOK]
        tile2d = lambda ap: ap.rearrange("p (a b) -> p a b", b=SIDE)
        half = lambda ap, c: ap[:, c * BANK:(c + 1) * BANK]
        NORM = {"0": (x_new[:, :], tile2d(x_new[:, :]), inner), "1": (x_new[:, :], x_new[:, :], h_mid),
                "2": (x_old[:, :], x_old[:, :], t0), "3": (x_old[:, :], x_old[:, :], t0)}

        gate_a, gate_s, xa, ml, xxy, um = (s64[:, i, :] for i in range(6))
        u2, z2, dt2, du2, sp2, yy2 = (m128[:, i, :] for i in range(6))
        mh = lambda ap: ap.rearrange("p (m t) -> p m t", m=MH)
        per_mh = lambda ap: ap.unsqueeze(2).broadcast_to([P, MH, SIDE])

        block = ctx.enter_context(nc.Block())
        last_base = bases("last", images - 1)
        finish_base = {e: last_base[e] + count(plans["last"], e) for e in "PADG"}

        def unit_of(u):
            return u // (2 * NST), u // NST % HALVES, u % NST

        def each_image(eng, body):
            body("first", 0)
            if images > 2:
                with eng.Fori(1, images - 1) as s:
                    body("mid", s)
            if images > 1:
                body("last", images - 1)

        def done(base, target):
            e, n = target
            return side[e], base[e] + n

        NONE = dict.fromkeys("PADG", 0)

        def lane_of(name):
            return int(name[1]) // 2

        def gn(name):
            return gn_lanes[:, lane_of(name), :]

        def stat(name):
            return gn(name)[:, 0:12].rearrange("p (i c) -> p i c", c=3)

        def lane_bank(name):
            return (w0, w1)[lane_of(name)]

        @block.sync
        def _(sp):
            sp.dma_start(wk[:, :], keep).then_inc(weights_in, 16)
            sp.dma_start(once_sb, once).then_inc(weights_in, 16)
            sp.dma_start(smallw[0:RANK, :], small).then_inc(weights_in, 16)
            sp.dma_start(dtw_sb[DTP:DTP + RANK, :], dtw).then_inc(weights_in, 16)
            sp.dma_start(conv_rows, conv_wt.partition_broadcast(P)).then_inc(weights_in, 16)
            sp.dma_start(preb[:, :], preb_row.partition_broadcast(P)).then_inc(weights_in, 16)
            sp.dma_start(q_sb[:, 0:3 * GATES], qw).then_inc(weights_in, 16)
            sp.dma_start(x_new[:, :], x_in[0]).then_inc(x_loaded, 16)
            sp.wait_ge(*done(NONE, nth(before, lead2_at - 1)))
            for c in range(2):
                k1 = kr[:, c * 512:c * 512 + 256].rearrange("p (a b) -> p a b", b=AMPS)
                k2 = kr[:, c * 512 + 256:c * 512 + 512].rearrange("p (a b) -> p a b", b=AMPS)
                sp.dma_start(lay[:, c * AMPS:(c + 1) * AMPS], k1).then_inc(matrices_in, 16)
                sp.dma_start(lay[:, (2 + c) * AMPS:(3 + c) * AMPS], k2).then_inc(matrices_in, 16)

            def spread_c(d, s, base, rows_done):
                sp.wait_ge(*done(base, rows_done))
                sp.dma_start(c_dram[d].rearrange("(n t) -> n t", t=TOK), c_rows).then_inc(c_out, 16)
                for g in range(NST // CGROUP):
                    if d or not (isinstance(s, int) and s == 0):
                        sp.wait_ge(prod_ready, s * UNITS + (2 * d - 1) * NST + (g + 1) * CGROUP)
                    if g == 0:
                        sp.wait_ge(c_out, 16 * (s * DIRS + d) + 16)
                    sp.dma_start(c_all[:, g * CGROUP:(g + 1) * CGROUP, :].rearrange("p n t -> p (n t)"),
                                 c_dram[d][g * CGROUP * TOK:(g + 1) * CGROUP * TOK].partition_broadcast(P)
                                 ).then_inc(c_in[g], 16)

            sp.wait_ge(*done(NONE, nth(before, begin_at - 1)))
            spread_c(0, 0, NONE, nth_named(before, ("dt_c_rows", 0, 1)))

            def image(kind, s):
                base = bases(kind, s)
                plan = plans[kind]
                for d in (1, 2):
                    spread_c(d, s, base, nth_named(plan, ("dt_c_rows", d, 1)))
                if kind != "first":
                    sp.wait_ge(*done(base, nth_named(plan, ("result", 1))))
                    sp.dma_start(out[s - 1], t0).then_inc(out_stored, 16)
                sp.dma_start(x_old[:, :], x_new[:, :]).then_inc(old_kept, 16)
                sp.dma_start(h_old[:, :], h_mid).then_inc(old_kept, 16)
                if kind != "last":
                    sp.wait_ge(old_kept, 32 * s + 32)
                    sp.dma_start(x_new[:, :], x_in[s + 1]).then_inc(x_loaded, 16)
                spread_c(3, s, base, nth_named(plan, ("dt_c_rows", 3, 1)))
                if kind != "last":
                    spread_c(0, s + 1, base, nth_named(plan, ("dt_c_rows", 0, 1)))

            each_image(sp, image)
            sp.wait_ge(*done(finish_base, nth_named(finish, ("result", 1))))
            sp.dma_start(out[images - 1], t0).then_inc(out_stored, 16)
            sp.wait_ge(out_stored, 16 * images)

        @block.gpsimd
        def _(pool):
            def step(name, s):
                k = name[0]
                if k == "zero":
                    pool.memset(padded[:, :, :], 0.0)
                    pool.memset(upad[:, :, :], 0.0)
                    pool.memset(neghalf[:, :], -0.5)
                    ins = pool.memset(h_new[:, :], 0.0)
                elif k == "bn_rstd":
                    r, b = (RANK, 2) if name[1] == "bn" else (P, ("bn1", "bn2").index(name[1]))
                    ins = pool.tensor_tensor(bnw[0:r, b, 1:2], bnw[0:r, b, 0:1], neghalf[0:r, :], ALU.pow)
                elif k == "group_rstd":
                    ins = pool.tensor_tensor(gn(name)[:, 19:20], gn(name)[:, 18:19], neghalf[:, :], ALU.pow)
                ins.then_inc(side["G"], 1)

            for i, (_, name, e, _) in enumerate(before):
                if e == "G":
                    if i:
                        pool.wait_ge(*done(NONE, step_before(before, i)))
                    step(name, 0)

            def image(kind, s):
                plan, base = plans[kind], bases(kind, s)
                for u in range(UNITS + 1):
                    if u < UNITS:
                        d, h, n = unit_of(u)
                        if h == 0 and n % CGROUP == 0:
                            pool.wait_ge(c_in[n // CGROUP], 16 * (s * DIRS + d) + 16)
                        pool.wait_ge(scan_done, s * UNITS + u + 1)
                        slot = ring[:, u % RING, :]
                        pool.tensor_tensor(slot, slot, c_all[:, n, :], ALU.mult).then_inc(prod_ready, 1)
                    for i, (at, name, e, _) in enumerate(plan):
                        if at == u and e == "G":
                            pool.wait_ge(*done(base, step_before(plan, i)))
                            step(name, s)

            each_image(pool, image)
            for i, (_, name, e, _) in enumerate(finish):
                if e == "G":
                    pool.wait_ge(*done(finish_base, step_before(finish, i)))
                    step(name, images)

        @block.scalar
        def _(act):
            def step(name, s):
                k = name[0]
                if k == "a_exp":
                    ins = act.activation(a_neg[:, :], kc("alog"), ACT.Exp)
                elif k == "a_exp2":
                    ins = act.activation(a_neg2[:, :], kc("alog2"), ACT.Exp)
                elif k == "q_sin":
                    ins = act.activation(sines, turns, ACT.Sin, scale=TWO_PI)
                elif k == "h1":
                    c = name[1]
                    if c == 0 and not (isinstance(s, int) and s == 0):
                        act.wait_ge(old_kept, 32 * s)
                    ins = act.activation(half(h_mid, c), w0, ACT.Relu, bias=bnw[:, 0, 4:5], scale=bnw[:, 0, 2:3])
                elif k in ("silu_exp", "silu_ln", "silu_inv"):
                    _, d, h, c, of = name
                    dst = half(u_conv[:, d % 2, h, :] if of == "u" else silu_z[:, h, :], c)
                    if k == "silu_ln":
                        ins = act.activation(dst, dst, ACT.Ln, bias=1.0)
                    elif k == "silu_inv":
                        ins = act.activation(dst, dst, ACT.Exp, scale=-1.0)
                    elif of == "u":
                        ins = act.activation(dst, w0, ACT.Exp, bias=conv_neg[:, h:h + 1], scale=-1.0)
                    else:
                        if not (isinstance(s, int) and s == 0 and d == 1):
                            act.wait_ge(y_taken, s * PASSES + d // 2 * 4)
                        ins = act.activation(dst, w0, ACT.Exp, scale=-1.0)
                elif k == "dt_c_rows":
                    _, d, c = name
                    if not (d == 0 and isinstance(s, int) and s == 0):
                        act.wait_ge(c_out, s * DIRS * 16 + d * 16)
                    ins = act.activation(half(dt_c_rows, c), w0[DTP:XP, :], ACT.Copy)
                elif k == "part":
                    _, d, i, c = name
                    r = slice(32 * i, 32 * i + 32)
                    ins = act.activation(half(stack[r, d % 2, :], c), w0[r, :], ACT.Copy)
                elif k == "dt_abs":
                    _, d, h, c = name
                    done = d * 2 * NST + (h - 1) * NST
                    if not isinstance(s, int) or s * UNITS + done > 0:
                        act.wait_ge(input_ready, s * UNITS + done)
                        act.wait_ge(decay_ready, s * UNITS + done)
                    ins = act.activation(half(du[:, h, :], c), w0, ACT.Abs, bias=kc("dt_b", h, h + 1))
                elif k == "dt_relu":
                    _, d, h, c = name
                    ins = act.activation(half(dt[:, h, :], c), w0, ACT.Relu, bias=kc("dt_b", h, h + 1))
                elif k == "dt_exp":
                    h = name[2]
                    ins = act.activation(du[:, h, :], du[:, h, :], ACT.Exp, scale=-1.0)
                elif k == "dt_ln":
                    h = name[2]
                    ins = act.activation(du[:, h, :], du[:, h, :], ACT.Ln, bias=1.0)
                elif k == "turned_y":
                    ins = act.activation(half(yz[:, name[2], name[3], :], name[4]), w1, ACT.Copy)
                elif k == "relu2":
                    ins = act.activation(half(t0, name[1]), w1, ACT.Relu, bias=bnw[:, 1, 4:5], scale=bnw[:, 1, 2:3])
                elif k == "squeeze_gelu":
                    ins = act.activation(g8[:, :], w1[0:RANK, 0:64], ACT.Gelu, bias=bnw[0:RANK, 2, 5:6],
                                         scale=bnw[0:RANK, 2, 2:3])
                elif k == "gate_tanh":
                    ins = act.activation(gate_s, gate_a, ACT.Tanh, scale=0.5)
                elif k == "silu2":
                    act.activation(u2, u2, ACT.Silu)
                    ins = act.activation(z2, z2, ACT.Silu)
                elif k == "dtabs2":
                    ins = act.activation(sp2, dt2, ACT.Abs)
                elif k == "dtrelu2":
                    ins = act.activation(dt2, dt2, ACT.Relu)
                elif k == "dtexp2":
                    ins = act.activation(sp2, sp2, ACT.Exp, scale=-1.0)
                elif k == "dtln2":
                    ins = act.activation(sp2, sp2, ACT.Ln, bias=1.0)
                elif k == "decay2":
                    ins = act.activation(t1[:, 0:512], t1[:, 0:512], ACT.Exp)
                elif k == "xa_tanh":
                    ins = act.activation(xa, xa, ACT.Tanh, scale=0.5)
                elif k == "mlp_gelu":
                    m = name[1]
                    ins = act.activation(ml[:, 32 * m:32 * m + 32], w1[:, 32 * m:32 * m + 32], ACT.Gelu,
                                         bias=kc("mlp1_b", m, m + 1))
                elif k == "sine":
                    ins = act.activation(circ[:, :, :, :].rearrange("p a j w -> p (a j w)"),
                                         circq[:, :, :, :].rearrange("p a j w -> p (a j w)"), ACT.Sin,
                                         scale=TWO_PI)
                elif k == "probability":
                    ins = act.activation(t1[:, 0:256], w1[:, 0:256], ACT.Square)
                ins.then_inc(side["A"], 1)
                if k in OTHER_TABLES:
                    act.preload_act_table_set("natural_log_exp_and_others")

            for i, (_, name, e, _) in enumerate(before):
                if e == "A":
                    if i:
                        act.wait_ge(*done(NONE, step_before(before, i)))
                    step(name, 0)

            def image(kind, s):
                plan, base = plans[kind], bases(kind, s)

                def decay(u):
                    d, h, n = unit_of(u)
                    if n == 0:
                        act.wait_ge(*done(base, nth_named(plan, ("dt_sum", d, h)) if u else ("D", 0)))
                    if u >= RING or not (isinstance(s, int) and s == 0):
                        act.wait_ge(sum_done, s * UNITS + u - RING + 1)
                    act.activation(ring[:, u % RING, :], dt[:, h, :], ACT.Exp,
                                   scale=a_neg[:, h * NST + n:h * NST + n + 1]).then_inc(decay_ready, 1)

                def take_y(p):
                    f, t, h = p // 4, p // 2 % 2, p % 2
                    if t == 0:
                        act.wait_ge(sum_done, s * UNITS + (p + 1) * NST)
                        if kind != "first":
                            act.wait_ge(*done(base, nth_named(plan, ("result", 1) if f else ("mix", 4, 1))))
                            if f:
                                act.wait_ge(out_stored, 16 * s)
                        act.activation(yz[:, f, h, :], y_acc[:, :], ACT.Copy).then_inc(y_taken, 1)

                decay(0)
                decay(1)
                for u in range(UNITS + 1):
                    for i, (at, name, e, _) in enumerate(plan):
                        if at == u and e == "A":
                            act.wait_ge(*done(base, step_before(plan, i)))
                            nxt = name[0] in ("h1",) or (len(name) > 1 and name[1] == 0
                                                         and name[0] in ("silu_exp", "silu_ln", "silu_inv", "dt_c_rows", "part")
                                                         or name[0][:3] == "dt_" and name[1:3] == (0, 0))
                            step(name, s + 1 if nxt else s)
                    if u % NST == 2 and u > 2:
                        take_y(u // NST - 1)
                    if u + 2 < UNITS:
                        decay(u + 2)
            each_image(act, image)
            for i, (_, name, e, _) in enumerate(finish):
                if e == "A":
                    act.wait_ge(*done(finish_base, step_before(finish, i)))
                    step(name, images)

        @block.vector
        def _(dve):
            MUL, ADD, SUB = ALU.mult, ALU.add, ALU.subtract

            def step(name, s):
                k = name[0]
                if k == "small_bf16":
                    dve.tensor_copy(negsel[0:96, :], kc("negstack")[0:96, :])
                    ins = dve.tensor_scalar(sel[0:96, :], kc("negstack")[0:96, :], -1.0, None, MUL)
                elif k == "conv_neg":
                    ins = dve.tensor_scalar(conv_neg[:, :], kc("conv_b"), -1.0, None, MUL)
                elif k == "fuse":
                    _, f, j = name
                    ins = dve.tensor_tensor(fused[:, f, j, :], oc("in", f * DI, (f + 1) * DI),
                                            conv_rows[:, j * DI:(j + 1) * DI], MUL)
                elif k == "diag":
                    h = name[1]
                    ins = dve.tensor_scalar(diag_d[:, h, :], kc("ident"), kc("D", h, h + 1), None, MUL)
                elif k == "a_neg":
                    ins = dve.tensor_scalar(a_neg[:, :], a_neg[:, :], -1.0, None, MUL)
                elif k == "a_neg2":
                    ins = dve.tensor_scalar(a_neg2[:, :], a_neg2[:, :], -1.0, None, MUL)
                elif k[:3] == "bn_" and len(name) > 1:
                    b = ("bn1", "bn2", "bn").index(name[1])
                    r = RANK if b == 2 else P
                    g = (lambda i: s8("bn", i, i + 1)) if b == 2 else (lambda i: kc(name[1], i, i + 1))
                    w = bnw[0:r, b, :]
                    if k == "bn_eps":
                        ins = dve.tensor_scalar(w[:, 0:1], g(3), 1e-5, None, ADD)
                    elif k == "bn_scale":
                        ins = dve.tensor_tensor(w[:, 2:3], w[:, 1:2], g(0), MUL)
                    elif k == "bn_ms":
                        ins = dve.tensor_tensor(w[:, 3:4], w[:, 2:3], g(2), MUL)
                    else:
                        ins = dve.tensor_tensor(w[:, 4:5], g(1), w[:, 3:4], SUB)
                elif k == "bn_bias":
                    ins = dve.tensor_tensor(bnw[0:RANK, 2, 6:7], bnw[0:RANK, 2, 2:3], s8("squeeze_b"), MUL)
                elif k == "bn_bias2":
                    ins = dve.tensor_tensor(bnw[0:RANK, 2, 5:6], bnw[0:RANK, 2, 4:5], bnw[0:RANK, 2, 6:7], ADD)
                elif k == "mixw_copy":
                    _, f, h = name
                    ins = dve.tensor_scalar(mixw[:, f, h, :], work[:, 0:P], 0.25, None, MUL)
                elif k == "q_sum":
                    ins = dve.tensor_tensor(q_tmp(0), angle(0), angle(2), ADD)
                elif k == "q_diff":
                    ins = dve.tensor_tensor(q_tmp(1), angle(0), angle(2), SUB)
                elif k == "q_quarter":
                    dve.tensor_scalar(qt(0, 0), angle(1), 0.5 / (2 * PI), None, MUL)
                    dve.tensor_scalar(qt(0, 1), angle(1), 0.5 / (2 * PI), 0.25, MUL, ADD)
                    for i in range(2):
                        dve.tensor_scalar(qt(1 + i, 0), q_tmp(i), 0.5 / (2 * PI), None, MUL)
                        ins = dve.tensor_scalar(qt(1 + i, 1), q_tmp(i), 0.5 / (2 * PI), 0.25, MUL, ADD)
                elif k == "q_up":
                    ins = dve.tensor_scalar(turns_whole, turns, ROUND, None, ADD)
                elif k == "q_down":
                    ins = dve.tensor_scalar(turns_whole, turns_whole, ROUND, None, SUB)
                elif k == "q_frac":
                    ins = dve.tensor_tensor(turns, turns, turns_whole, SUB)
                elif k == "gate":
                    e, c = divmod(name[1], 2)
                    trig, ang = (qs(0, 1), 1) if e in (0, 3) else (qs(0, 0), 2)
                    other = qs(ang, 1 - c)
                    sign = {(0, 1): -1.0, (1, 0): -1.0, (1, 1): -1.0, (2, 1): -1.0}.get((e, c), 1.0)
                    dst = gate_m[:, c * 32:c * 32 + 32].rearrange("p (g e) -> p g e", e=4)[:, :, e]
                    ins = dve.scalar_tensor_tensor(out=dst, in0=trig, scalar=sign, in1=other, op0=MUL, op1=MUL)
                elif k == "gate_negs":
                    ins = dve.tensor_scalar(gate_m[:, 64:96], gate_m[:, 32:64], -1.0, None, MUL)
                elif k == "kron":
                    ins = kron(name[1], name[2])
                elif k == "m1_copy":
                    ins = dve.tensor_copy(m1, work[0:AMPS, 0:4 * AMPS])
                elif k == "q_neg":
                    ins = dve.tensor_scalar(q_neg, m1[:, 3 * AMPS:4 * AMPS], -1.0, None, MUL)
                elif k == "tt_copy":
                    ins = dve.tensor_copy(ttc, work[0:AMPS, 0:2 * AMPS])
                elif k == "blocks_mask":
                    c = name[1]
                    ins = dve.tensor_tensor(
                        unitary[:, c, :].rearrange("p (j k) -> p j k", k=AMPS),
                        kc("rowmask").unsqueeze(2).broadcast_to([P, CH, AMPS]),
                        work[:, c * AMPS:(c + 1) * AMPS].unsqueeze(1).broadcast_to([P, CH, AMPS]), MUL)
                elif k == "postw_mask":
                    j = name[1]
                    ins = dve.tensor_scalar(postw[:, j, :], work[:, 0:P], kc("rowmask", j, j + 1), None, MUL)
                elif k == "stats":
                    src = NORM[name[1]][0]
                    if name[1] == "0":
                        dve.wait_ge(x_loaded, 16 * s + 16)
                    h = name[2]
                    ins = dve.bn_stats(gn(name)[:, 6 * h:6 * h + 6], src[:, 512 * h:512 * h + 512])
                elif k == "square":
                    ins = dve.tensor_tensor(gn(name)[:, 21:25], stat(name)[:, :, 1], stat(name)[:, :, 1], MUL)
                elif k == "mean_square":
                    ins = dve.scalar_tensor_tensor(out=stat(name)[:, :, 2], in0=stat(name)[:, :, 2], scalar=4.0 / TOK,
                                                   in1=gn(name)[:, 21:25], op0=MUL, op1=ADD)
                elif k == "group_copy":
                    ins = dve.tensor_reduce(gn(name)[:, 14:16],
                                            lane_bank(name)[:, 0:12].rearrange("p (i c) -> p c i", c=3)[:, 1:3, :],
                                            AX.X, ADD)
                elif k == "group_negvar":
                    ins = dve.scalar_tensor_tensor(out=gn(name)[:, 17:18], in0=gn(name)[:, 14:15], scalar=gn(name)[:, 14:15],
                                                   in1=gn(name)[:, 15:16], op0=MUL, op1=SUB)
                elif k == "group_eps":
                    ins = dve.tensor_scalar(gn(name)[:, 18:19], gn(name)[:, 17:18], -1.0, 1e-5, MUL, ADD)
                elif k == "group_shift":
                    ins = dve.scalar_tensor_tensor(out=gn(name)[:, 20:21], in0=gn(name)[:, 14:15], scalar=-1.0,
                                                   in1=gn(name)[:, 19:20], op0=MUL, op1=MUL)
                elif k == "norm":
                    _, src, dst = NORM[name[1]]
                    if name[1] == "1" and not (isinstance(s, int) and s == 0):
                        dve.wait_ge(old_kept, 32 * s)
                    ins = dve.tensor_scalar(dst, src, gn(name)[:, 19:20], gn(name)[:, 20:21], MUL, ADD)
                elif k == "add0":
                    x = half(x_new, name[1])
                    ins = dve.scalar_tensor_tensor(out=x, in0=w0, scalar=kc("conv0_b"), in1=x, op0=ADD, op1=ADD)
                elif k == "silu_u":
                    _, d, h, c = name
                    u = half(u_conv[:, d % 2, h, :], c)
                    ins = dve.scalar_tensor_tensor(out=u, in0=w0, scalar=kc("conv_b", h, h + 1), in1=u, op0=ADD,
                                                   op1=MUL)
                elif k == "silu_z":
                    _, d, h, c = name
                    z = half(silu_z[:, h, :], c)
                    ins = dve.tensor_tensor(z, z, w0, MUL)
                elif k == "dt_sum":
                    h = name[2]
                    ins = dve.tensor_tensor(dt[:, h, :], dt[:, h, :], du[:, h, :], ADD)
                elif k == "dt_u":
                    _, d, h = name
                    ins = dve.tensor_tensor(du[:, h, :], dt[:, h, :], u_conv[:, d % 2, h, :], MUL)
                elif k == "add1":
                    ins = dve.tensor_tensor(x_old[:, :], x_old[:, :], t0, ADD)
                elif k == "rows":
                    ins = dve.tensor_reduce(um[:, 0:32], tile2d(t0), AX.X, ADD)
                elif k == "cols":
                    ins = dve.tensor_reduce(um[:, 32:64], t0.rearrange("p (a b) -> p b a", b=SIDE), AX.X, ADD)
                elif k == "means":
                    ins = dve.tensor_scalar(um, um, 1.0 / SIDE, None, MUL)
                elif k in ("gate_h", "gate_w"):
                    i = k == "gate_w"
                    ins = dve.tensor_scalar(gate_a[:, 32 * i:32 * i + 32], w1[:, 32 * i:32 * i + 32],
                                            kc("gate_b", int(i), i + 1), None, ADD)
                elif k == "gate_sig":
                    ins = dve.tensor_scalar(gate_s, gate_s, 0.5, 0.5, MUL, ADD)
                elif k == "pad2":
                    ins = dve.tensor_copy(upad[:, :, PAD:PAD + SIDE], mh(w1[:, 0:128]))
                elif k == "z2":
                    ins = dve.tensor_copy(z2, w1[:, 128:256])
                elif k == "taps2":
                    w4 = kc("taps2").rearrange("p (m k) -> p m k", k=TAPS)
                    for i in range(MH):
                        ins = dve.tensor_tensor(
                            t1[:, 128 * i:128 * i + 128].rearrange("p (k t) -> p k t", k=TAPS),
                            windows(i), w4[:, i, :].unsqueeze(2).broadcast_to([P, TAPS, SIDE]), MUL)
                elif k == "tapsum2":
                    ins = dve.tensor_reduce(mh(u2), t1[:, 0:512].rearrange("p (m k t) -> p m t k", m=MH, k=TAPS),
                                            AX.X, ADD)
                elif k == "tapbias2":
                    ins = dve.tensor_tensor(mh(u2), mh(u2), per_mh(kc("conv2_b")), ADD)
                elif k == "xcopy2":
                    ins = dve.tensor_copy(dbl[:, :], w1[0:XP2, 0:64])
                elif k == "dtbias2":
                    ins = dve.tensor_tensor(mh(dt2), mh(w1[:, 0:128]), per_mh(kc("dt2_b")), ADD)
                elif k == "dtsum2":
                    ins = dve.tensor_tensor(dt2, dt2, sp2, ADD)
                elif k == "du2":
                    ins = dve.tensor_tensor(du2, dt2, u2, MUL)
                elif k in ("dta2", "start2", "input2", "scan2", "prod2", "ysum2"):
                    _, m, h = name
                    i = 2 * m + h
                    a, b = t1[:, 0:512], t1[:, 512:1024]
                    nt = lambda ap: ap.rearrange("p (n t) -> p n t", t=SIDE)
                    over_n = lambda ap: mh(ap)[:, i, :].unsqueeze(1).broadcast_to([P, NST, SIDE])
                    if k == "dta2":
                        ins = dve.tensor_tensor(
                            nt(a), over_n(dt2),
                            a_neg2[:, i * NST:(i + 1) * NST].unsqueeze(2).broadcast_to([P, NST, SIDE]), MUL)
                    elif k == "start2":
                        ins = dve.memset(nt(a)[:, :, 0], 0.0)
                    elif k == "input2":
                        ins = dve.tensor_tensor(nt(b), over_n(du2), nt(w1), MUL)
                    elif k == "scan2":
                        ins = dve.tensor_tensor_scan(a, a, b, 0.0, MUL, ADD)
                    elif k == "prod2":
                        ins = dve.tensor_tensor(b, a, w1, MUL)
                    else:
                        ins = dve.tensor_reduce(mh(yy2)[:, i, :], b.rearrange("p (n t) -> p t n", t=SIDE), AX.X, ADD)
                elif k == "dterm2":
                    ins = dve.tensor_tensor(mh(sp2), mh(u2), per_mh(kc("D2")), MUL)
                elif k == "dadd2":
                    ins = dve.tensor_tensor(yy2, yy2, sp2, ADD)
                elif k == "yz2":
                    ins = dve.tensor_tensor(yy2, yy2, z2, MUL)
                elif k == "xa":
                    ins = dve.tensor_tensor(xa, w1[:, 0:64], gate_a, ADD)
                elif k == "xa_sig":
                    ins = dve.tensor_scalar(xa, xa, 0.5, 0.5, MUL, ADD)
                elif k == "mlp_b":
                    m = name[1]
                    ins = dve.tensor_scalar(xxy[:, 32 * m:32 * m + 32], w1[:, 32 * m:32 * m + 32],
                                            kc("mlp2_b", m, m + 1), None, ADD)
                elif k == "outer_h":
                    ins = dve.tensor_tensor(tile2d(t1), gate_s[:, 0:32].unsqueeze(2).broadcast_to([P, SIDE, SIDE]),
                                            xxy[:, 32:64].unsqueeze(1).broadcast_to([P, SIDE, SIDE]), MUL)
                elif k == "outer_w":
                    ins = dve.tensor_tensor(inner, gate_s[:, 32:64].unsqueeze(1).broadcast_to([P, SIDE, SIDE]),
                                            xxy[:, 0:32].unsqueeze(2).broadcast_to([P, SIDE, SIDE]), MUL)
                elif k == "times_x":
                    ins = dve.tensor_tensor(half(t0, name[1]), half(t0, name[1]), w1, MUL)
                elif k == "add2":
                    ins = dve.tensor_tensor(x_old[:, :], x_old[:, :], t0, ADD)
                elif k == "angle_b":
                    ins = dve.tensor_tensor(circq[:, 0, :, :],
                                            w1[:, 0:CH * NQ].rearrange("p (j w) -> p j w", w=NQ),
                                            preb[:, :].unsqueeze(1).broadcast_to([P, CH, NQ]), ADD)
                elif k == "turns":
                    i = name[1]
                    ins = dve.tensor_scalar(circ[:, i, :, :], circq[:, 0, :, :], 0.25, 0.25 * (1 - i), MUL, ADD)
                elif k == "round_up":
                    ins = dve.tensor_scalar(circq[:, :, :, :], circ[:, :, :, :], ROUND, None, ADD)
                elif k == "round_down":
                    ins = dve.tensor_scalar(circq[:, :, :, :], circq[:, :, :, :], ROUND, None, SUB)
                elif k == "fraction":
                    ins = dve.tensor_tensor(circq[:, :, :, :], circ[:, :, :, :], circq[:, :, :, :], SUB)
                elif k == "pair":
                    i = name[1]
                    a = circ[:, :, :, 2 * i].rearrange("p b j -> p j b").unsqueeze(3).broadcast_to([P, CH, 2, 2])
                    b = circ[:, :, :, 2 * i + 1].rearrange("p b j -> p j b").unsqueeze(2).broadcast_to([P, CH, 2, 2])
                    ins = dve.tensor_tensor(sp2[:, 32 * i:32 * i + 32].rearrange("p (j a b) -> p j a b", a=2, b=2),
                                            a, b, MUL)
                elif k == "amplitudes":
                    a = sp2[:, 0:32].rearrange("p (j a) -> p j a", a=4).unsqueeze(3).broadcast_to([P, CH, 4, 4])
                    b = sp2[:, 32:64].rearrange("p (j a) -> p j a", a=4).unsqueeze(2).broadcast_to([P, CH, 4, 4])
                    ins = dve.tensor_tensor(yy2.rearrange("p (j a b) -> p j a b", a=4, b=4), a, b, MUL)
                elif k == "turn_copy":
                    ins = dve.tensor_copy(du2, w1[:, 0:P])
                elif k == "result":
                    c = name[1]
                    ins = dve.scalar_tensor_tensor(out=half(t0, c), in0=w1, scalar=kc("post_b"),
                                                   in1=half(x_old, c), op0=ADD, op1=ADD)
                ins.then_inc(side["D"], 1)

            def windows(i):
                ap = upad[:, i, 0:SIDE].unsqueeze(1).broadcast_to([P, TAPS, SIDE])
                return bass.AP(ap.tensor, ap.offset, [ap.ap[0], [1, TAPS], [1, SIDE]])

            def angle(i):
                return q_sb[:, 0:3 * GATES].rearrange("p (g a) -> p g a", a=3)[:, :, i]

            def q_tmp(i):
                return q_sb[:, 24 + 8 * i:32 + 8 * i]

            def qt(i, c):
                return q_sb[:, 48 + 16 * i + 8 * c:56 + 16 * i + 8 * c]

            def qs(i, c):
                return sines[:, 16 * i + 8 * c:16 * i + 8 * c + 8]

            def kron(n, part):
                ins = None
                for layer in range(2):
                    if n < 2:
                        size = 2
                        g = 4 * layer + 2 * n
                        a = lambda c: gate_m[:, c * 32 + 4 * g:c * 32 + 4 * g + 4]
                        b = lambda c: gate_m[:, c * 32 + 4 * g + 4:c * 32 + 4 * g + 8]
                        o = (kr01, kr23)[n]
                        dst = lambda c: o[:, c * 32 + 16 * layer:c * 32 + 16 * layer + 16]
                        tmp = krt[:, 64 + 32 * layer:64 + 32 * layer + 32]
                    else:
                        size = 4
                        a = lambda c: kr01[:, c * 32 + 16 * layer:c * 32 + 16 * layer + 16]
                        b = lambda c: kr23[:, c * 32 + 16 * layer:c * 32 + 16 * layer + 16]
                        dst = lambda c: kr[:, c * 512 + 256 * layer:c * 512 + 256 * layer + 256]
                        tmp = scratch[0:1, 5632 + 512 * layer:5632 + 512 * layer + 512]
                    half = size ** 4

                    def times(out_ap, x, y):
                        o4 = out_ap.rearrange("p (i k j l) -> p i k j l", i=size, k=size, j=size)
                        x2 = x.rearrange("p (i j) -> p i j", j=size)
                        y2 = y.rearrange("p (k l) -> p k l", l=size)
                        last = None
                        for i in range(size):
                            last = dve.tensor_tensor(
                                o4[:, i], x2[:, i, :].unsqueeze(1).unsqueeze(3).broadcast_to([1, size, size, size]),
                                y2.unsqueeze(2).broadcast_to([1, size, size, size]), MUL)
                        return last

                    if part == 0:
                        times(dst(0), a(0), b(0))
                        ins = times(dst(1), a(0), b(1))
                    elif part == 1:
                        times(tmp[:, 0:half], a(1), b(1))
                        ins = times(tmp[:, half:2 * half], a(1), b(0))
                    else:
                        dve.tensor_tensor(dst(0), dst(0), tmp[:, 0:half], SUB)
                        ins = dve.tensor_tensor(dst(1), dst(1), tmp[:, half:2 * half], ADD)
                return ins

            dve.wait_ge(weights_in, 16 * 7)

            for i, (_, name, e, _) in enumerate(before):
                if e == "D":
                    if i:
                        dve.wait_ge(*done(NONE, step_before(before, i)))
                    step(name, 0)

            def image(kind, s):
                plan, base = plans[kind], bases(kind, s)

                def take_y(p):
                    f, t, h = p // 4, p // 2 % 2, p % 2
                    if t:
                        dve.wait_ge(sum_done, s * UNITS + (p + 1) * NST)
                        dve.tensor_tensor(yz[:, f, h, :], y_acc[:, :], silu_z[:, h, :], MUL).then_inc(y_taken, 1)

                for u in range(UNITS + 1):
                    if u < UNITS:
                        d, h, n = unit_of(u)
                        if n == 0:
                            dve.wait_ge(*done(base, nth_named(plan, ("dt_u", d, h)) if u else ("D", 0)))
                        dve.wait_ge(b_ready, s * UNITS + u + 1)
                        b = bring[:, u % BRING, :]
                        dve.tensor_tensor(b, du[:, h, :], b, MUL).then_inc(input_ready, 1)
                        dve.wait_ge(input_ready, s * UNITS + u + 1)
                        dve.wait_ge(decay_ready, s * UNITS + u + 1)
                        slot = ring[:, u % RING, :]
                        if d % 2:
                            slot, b = slot[:, ::-1], b[:, ::-1]
                        dve.tensor_tensor_scan(slot, slot, b, 0.0, MUL, ADD).then_inc(scan_done, 1)
                    for i, (at, name, e, _) in enumerate(plan):
                        if at == u and e == "D":
                            dve.wait_ge(*done(base, step_before(plan, i)))
                            step(name, s + 1 if name in [x[0] for x in front()] else s)
                    if u % NST == 1 and u > 1:
                        take_y(u // NST - 1)
                    if u == UNITS:
                        take_y(PASSES - 1)
            each_image(dve, image)
            for i, (_, name, e, _) in enumerate(finish):
                if e == "D":
                    dve.wait_ge(*done(finish_base, step_before(finish, i)))
                    step(name, images)

        @block.tensor
        def _(pe):
            def mm(out_ap, w, x, start, stop):
                return pe.matmul(out_ap, w, x, start=start, stop=stop, skip_group_check=True)

            def halves(out_t, w, x, start, stop):
                for c in range(2):
                    ins = mm(half(out_t, c), w, half(x, c), start, stop)
                return ins

            def chunk(ap, j):
                return ap[:, j * P:(j + 1) * P]

            def turn(out_t, x, start, stop, chunks=CH):
                for j in range(chunks):
                    ins = pe.matmul(chunk(out_t, j), chunk(x, j), kc("ident"), is_transpose=True,
                                    start=start and j % (BANK // P) == 0, stop=stop, skip_group_check=True)
                return ins

            def step(name, s):
                k = name[0]
                if k == "mixw":
                    _, f, h = name
                    ins = mm(work[:, 0:P], oc("outp", f * DI + h * P, f * DI + (h + 1) * P), kc("nin2"), True, True)
                elif k == "m1":
                    pe.wait_ge(matrices_in, 16 * 4)
                    for c in range(2):
                        mm(work[0:AMPS, c * AMPS:(c + 1) * AMPS], oc("perm1", rows=AMPS),
                           lay[:, c * AMPS:(c + 1) * AMPS], True, True)
                        ins = mm(work[0:AMPS, (2 + c) * AMPS:(3 + c) * AMPS],
                                 lay[:, (2 + c) * AMPS:(3 + c) * AMPS], oc("perm2", rows=AMPS), True, True)
                elif k == "tt":
                    m = [m1[:, i * AMPS:(i + 1) * AMPS] for i in range(4)]
                    mm(work[0:AMPS, 0:AMPS], m[0], m[2], True, False)
                    mm(work[0:AMPS, 0:AMPS], m[1], q_neg, False, True)
                    mm(work[0:AMPS, AMPS:2 * AMPS], m[0], m[3], True, False)
                    ins = mm(work[0:AMPS, AMPS:2 * AMPS], m[1], m[2], False, True)
                elif k == "blocks":
                    ins = mm(work[:, 0:2 * AMPS], oc("rep", rows=AMPS), ttc, True, True)
                elif k == "postw":
                    ins = mm(work[:, 0:P], oc("sign", rows=NQ), oc("post", rows=NQ), True, True)
                elif k == "group_mean":
                    ins = mm(lane_bank(name)[:, 0:12], kc("gavg"), gn(name)[:, 0:12], True, True)
                elif k == "conv0":
                    _, tap, c = name
                    i, j = divmod(tap, 3)
                    ins = mm(w0, kc("conv0", tap * P, (tap + 1) * P),
                             padded[:, i + 16 * c:i + 16 * c + 16, j:j + SIDE], tap == 0, tap == 8)
                elif k == "nin":
                    ins = mm(w0, kc("nin"), half(h_mid, name[1]), True, True)
                elif k == "conv_in":
                    _, d, h, j, c = name
                    off = (2 * PAD - j if d % 2 else j) + c * BANK
                    ins = mm(w0, fused[:, d // 2, j, h * P:(h + 1) * P], h_new[:, off:off + BANK],
                             j == 0, j == TAPS - 1)
                elif k == "z":
                    _, d, h, c = name
                    lo = d // 2 * DI + h * P
                    for j in range(BANK // P):
                        ins = mm(chunk(w0, j), chunk(half(h_mid, c), j), kc("z", lo, lo + P), j == 0, True)
                elif k == "xproj":
                    _, d, c, h = name
                    ins = mm(w0[0:XP, :], kc("xproj", h * XP, (h + 1) * XP), half(u_conv[:, d % 2, h, :], c),
                             h == 0, h == HALVES - 1)
                elif k == "rest":
                    _, d, i, c = name
                    r = slice(32 * i, 32 * i + 32)
                    ins = mm(w0[0:96, :], negsel[r, :], half(stack[r, d % 2, :], c), False, True)
                elif k == "dt_proj":
                    _, d, h, c = name
                    ins = mm(w0, dtw_sb[DTP:DTP + RANK, h * P:(h + 1) * P], half(dt_rows, c), True, True)
                elif k == "turn_y":
                    _, which, f, h, c = name
                    if c == 0:
                        pe.wait_ge(y_taken, (s - (which == "before")) * PASSES + 4 * f + 3 + h)
                    ins = turn(w1, half(yz[:, f, h, :], c), True, True, BANK // P)
                elif k == "mix":
                    _, i, c = name
                    if i < 4:
                        ins = mm(w1, mixw[:, i // 2, i % 2, :], half(yz[:, i // 2, i % 2, :], c), i == 0, False)
                    else:
                        pe.wait_ge(old_kept, 32 * s)
                        ins = mm(w1, kc("nin2"), half(h_old, c), False, True)
                elif k == "squeeze":
                    ins = mm(w1[0:RANK, 0:64], kc("squeeze"), um, True, True)
                elif k == "gates":
                    mm(w1[:, 0:32], s8("spread_h"), g8[:, 0:32], True, True)
                    ins = mm(w1[:, 32:64], s8("spread_w"), g8[:, 32:64], True, True)
                elif k == "in2":
                    for m in range(2):
                        for i in range(4):
                            h = i % 2
                            col = (i // 2) * 128 + (2 * m + h) * 32
                            ins = mm(w1[:, col:col + 32], kc("in2", m * 2 * DI + i * P, m * 2 * DI + (i + 1) * P),
                                     um[:, 32 * m:32 * m + 32], True, True)
                elif k == "xproj2":
                    for m in range(2):
                        for h in range(HALVES):
                            i = 2 * m + h
                            ins = mm(w1[0:XP2, 32 * m:32 * m + 32], kc("xproj2", i * XP2, (i + 1) * XP2),
                                     mh(u2)[:, i, :], h == 0, h == 1)
                elif k == "dtproj2":
                    for i in range(MH):
                        ins = mm(w1[:, 32 * i:32 * i + 32], s8("dtp2", i * P, (i + 1) * P),
                                 dbl[0:RANK, 32 * (i // 2):32 * (i // 2) + 32], True, True)
                elif k == "spread2":
                    _, m, _, which = name
                    for n in range(NST):
                        row = RANK + which * NST + n
                        ins = mm(w1[:, SIDE * n:SIDE * n + SIDE],
                                 kc("ident", row, row + 1)[0:XP2, :].broadcast_to([XP2, P]),
                                 dbl[:, SIDE * m:SIDE * m + SIDE], True, True)
                elif k == "out2":
                    for m in range(2):
                        for h in range(HALVES):
                            i = 2 * m + h
                            ins = mm(w1[:, 32 * m:32 * m + 32], kc("out2", i * P, (i + 1) * P), mh(yy2)[:, i, :],
                                     h == 0, h == 1)
                elif k in ("mlp1", "mlp2"):
                    src = xa if k == "mlp1" else ml
                    for m, a in enumerate("xy"):
                        ins = mm(w1[:, 32 * m:32 * m + 32], kc(k + a), src[:, 32 * m:32 * m + 32], True, True)
                elif k == "adjust":
                    _, i, c = name
                    ins = mm(w1, kc("adjust", i * P, (i + 1) * P), inner[:, 16 * c:16 * c + 16, :] if i else half(t1, c),
                             i == 0, i == 1)
                elif k == "angles":
                    for j in range(CH):
                        ins = mm(w1[:, NQ * j:NQ * j + NQ], t0[:, j * P:(j + 1) * P], kc("pre"), True, True)
                elif k == "turn":
                    ins = mm(w1[:, 0:P], yy2, kc("ident"), True, True)
                elif k == "unitary":
                    for c in range(2):
                        ins = mm(w1[:, c * P:(c + 1) * P], unitary[:, c, :], du2, True, True)
                elif k == "post":
                    for j in range(BANK // P):
                        for c in range(2):
                            ins = mm(chunk(w1, j), postw[:, 4 * name[1] + j, :], chunk(t1, c), c == 0, c == 1)
                ins.then_inc(side["P"], 1)

            for i, (_, name, e, _) in enumerate(before):
                if e == "P":
                    if i:
                        pe.wait_ge(*done(NONE, step_before(before, i)))
                    step(name, 0)

            def image(kind, s):
                plan, base = plans[kind], bases(kind, s)

                def spread_b(u):
                    d, h, n = unit_of(u)
                    if h == 0 and n == 0:
                        pe.wait_ge(*done(base, nth_named(plan, ("part", d, 2, 1)) if u else ("D", 0)))
                    if u >= BRING or not (isinstance(s, int) and s == 0):
                        pe.wait_ge(scan_done, s * UNITS + u - BRING + 1)
                    halves(bring[:, u % BRING, :], sel[0:96, n:n + 1].broadcast_to([96, P]),
                           stack[0:96, d % 2, :], True, True).then_inc(b_ready, 1)

                def add_y(u):
                    d, h, n = unit_of(u)
                    if n == 0 and (u or not (isinstance(s, int) and s == 0)):
                        pe.wait_ge(y_taken, s * PASSES + u // NST)
                    if n == 3:
                        for j in range(CH):
                            mm(chunk(y_acc, j), chunk(u_conv[:, d % 2, h, :], j), diag_d[:, h, :], False, False)
                    if n == 5 and d % 2:
                        halves(y_acc, kc("ident"), yz[:, d // 2, h, :], False, False)
                    pe.wait_ge(prod_ready, s * UNITS + u + 1)
                    turn(y_acc, ring[:, u % RING, :], n == 0, n == NST - 1).then_inc(sum_done, 1)

                spread_b(0)
                for u in range(UNITS + 1):
                    if u + 1 < UNITS:
                        spread_b(u + 1)
                    for i, (at, name, e, _) in enumerate(plan):
                        if at == u and e == "P":
                            pe.wait_ge(*done(base, step_before(plan, i)))
                            step(name, s)
                    if 2 <= u < UNITS:
                        add_y(u - 2)
                    if u == UNITS:
                        add_y(UNITS - 2)
                        add_y(UNITS - 1)
            each_image(pe, image)
            for i, (_, name, e, _) in enumerate(finish):
                if e == "P":
                    pe.wait_ge(*done(finish_base, step_before(finish, i)))
                    step(name, images)


def layout(inp):
    a = {k: np.asarray(v) for k, v in inp.items()}
    L1 = {k[8:]: v for k, v in a.items() if k.startswith("L1_conv_")}
    L2 = {k[8:]: v for k, v in a.items() if k.startswith("L2_conv_")}
    L3 = {k[8:]: v for k, v in a.items() if k.startswith("L3_conv_")}
    col = lambda v: v.reshape(-1, P).T
    eye = np.eye(P, dtype=np.float32)
    w_in = L1["in_proj_w"].T
    xp = L1["x_proj_w"].T
    xproj = []
    for h in range(HALVES):
        r = xp[h * P:(h + 1) * P]
        b_pad = np.concatenate([r[:, RANK:RANK + NST], np.zeros((P, 32 - NST), np.float32)], axis=1)
        xproj += [b_pad] * PARTS + [r[:, :RANK], r[:, RANK + NST:]]
    halfcols = lambda m: [m[h * P:(h + 1) * P] for h in range(HALVES)]
    neg = np.zeros((P, 96), np.float32)
    for i in range(96):
        for j in range(3):
            neg[i, i % 32 + 32 * j] = -1.0
    keep = {
        "conv0": [a["L0_conv_weight"].transpose(1, 2, 3, 0).reshape(P, 9 * P)],
        "nin": [L1["nin_w"].T], "z": [w_in[:, DI:], w_in[::-1, DI:]], "xproj": xproj,
        "nin2": [L1["nin2_w"].T], "ident": [eye],
        "gavg": [np.kron(np.eye(P // GROUP, dtype=np.float32), np.full((GROUP, GROUP), 1 / (4 * GROUP), np.float32))],
        "alog": halfcols(L1["A_log"]), "conv0_b": [col(a["L0_conv_bias"])], "conv_b": [col(L1["conv_b"])],
        "dt_b": [col(L1["dt_proj_b"])], "D": [col(L1["D"])],
        "bn1": [col(L1["bn1_" + k]) for k in "gbmv"], "bn2": [col(L1["bn2_" + k]) for k in "gbmv"],
        "squeeze": [L2["conv1_w"].T], "mlp1x": [L2["mlpx_w1"].T], "mlp1y": [L2["mlpy_w1"].T],
        "mlp2x": [L2["mlpx_w2"].T], "mlp2y": [L2["mlpy_w2"].T],
        "adjust": [L2["adjust_w"][:, :P].T, L2["adjust_w"][:, P:].T],
        "in2": [L2["mx_in_w"].T, L2["my_in_w"].T],
        "taps2": [m for w in ("mx", "my") for m in halfcols(L2[w + "_conv_w"][:, 0])],
        "conv2_b": [col(L2["mx_conv_b"]), col(L2["my_conv_b"])],
        "xproj2": [m for w in ("mx", "my") for m in halfcols(L2[w + "_xproj_w"].T)],
        "dt2_b": [col(L2["mx_dt_b"]), col(L2["my_dt_b"])],
        "alog2": [m for w in ("mx", "my") for m in halfcols(L2[w + "_Alog"])],
        "D2": [col(L2["mx_D"]), col(L2["my_D"])],
        "out2": [m for w in ("mx", "my") for m in halfcols(L2[w + "_out_w"].T)],
        "gate_b": [col(L2["convh_b"]), col(L2["convw_b"])],
        "mlp1_b": [col(L2["mlpx_b1"]), col(L2["mlpy_b1"])], "mlp2_b": [col(L2["mlpx_b2"]), col(L2["mlpy_b2"])],
        "pre": [L3["pre_w"].T], "post_b": [col(L3["post_b"])], "negstack": [neg],
        "rowmask": [np.kron(np.eye(CH, dtype=np.float32), np.ones((AMPS, 1), np.float32))],
    }

    def tall(m):
        out = np.zeros((P, m.shape[1]), np.float32)
        out[:m.shape[0]] = m
        return out

    def perm_t(layer):
        m = np.zeros((AMPS, AMPS), np.float32)
        for k, to in enumerate(circuit_entangler(layer)):
            m[k, to] = 1.0
        return m

    sign = np.array([[1.0 - 2.0 * (i % AMPS >> NQ - 1 - w & 1) for i in range(P)] for w in range(NQ)], np.float32)
    once = {
        "in": [w_in[:, :DI], w_in[::-1, :DI]], "outp": [L1["out_proj_w"], L1["out_proj_w"][::-1]],
        "perm1": [tall(perm_t(0))], "perm2": [tall(perm_t(1))],
        "rep": [tall(np.tile(np.eye(AMPS, dtype=np.float32), (1, CH)))], "sign": [tall(sign)],
        "post": [tall(L3["post_w"].T)],
    }
    small = {
        "spread_h": [L2["convh_w"].T], "spread_w": [L2["convw_w"].T],
        "dtp2": [L2["mx_dt_w"].T, L2["my_dt_w"].T], "bn": [L2["bn_" + k][:, None] for k in "gbmv"],
        "squeeze_b": [L2["conv1_b"][:, None]],
    }
    pack = lambda table, parts: np.ascontiguousarray(
        np.concatenate([m for name, _ in table for m in parts[name]], axis=1))
    return {
        "x": a["x"].reshape(a["x"].shape[0], P, TOK), "keep": pack(KEEP, keep), "once": pack(ONCE, once),
        "small": pack(SMALL, small), "dtw": np.ascontiguousarray(L1["dt_proj_w"].T),
        "conv_wt": np.ascontiguousarray(L1["conv_w"].T).reshape(TAPS * DI),
        "preb": L3["pre_b"], "qw": L3["q_weights"].reshape(1, -1),
    }


def kernel(**inputs):
    import concourse.bacc as bacc
    from concourse.bass_utils import run_bass_kernel_spmd

    laid = layout(inputs)
    images = laid["x"].shape[0]
    nc = bacc.Bacc("TRN2", target_bir_lowering=False, num_devices=1)
    arrays = {f"in_{k}": v for k, v in laid.items()}
    aps = {k: nc.dram_tensor(f"in_{k}", list(v.shape), F32, kind="ExternalInput").ap() for k, v in laid.items()}
    out = nc.dram_tensor("out_0", [images, P, TOK], F32, kind="ExternalOutput").ap()
    four_layers(nc, images, aps["x"], aps["keep"], aps["once"], aps["small"], aps["dtw"], aps["conv_wt"],
                aps["preb"], aps["qw"], out)
    r = run_bass_kernel_spmd(nc, [arrays], core_ids=[0])
    return np.asarray(r.results[0]["out_0"]).reshape(images, P, SIDE, SIDE)
```
